# Optimizing a Trainium2 kernel written in Bass

```python
import numpy as np
import jax
import jax.numpy as jnp

def _softmax(x, axis=-1):
    return jax.nn.softmax(x, axis=axis)

def _gelu(x):
    return jax.nn.gelu(x, approximate=True)

def _silu(x):
    return jax.nn.silu(x)

def _sigmoid(x):
    return jax.nn.sigmoid(x)

def _layernorm(x, axis=-1, eps=1e-05):
    m = jnp.mean(x, axis=axis, keepdims=True)
    v = jnp.var(x, axis=axis, keepdims=True)
    return (x - m) / jnp.sqrt(v + eps)

def _scatter_add(tgt, idx, src, axis=0):
    return tgt.at[idx].add(src)

def _segment_sum(src, seg, n):
    return jax.ops.segment_sum(src, seg, n)
kernel_name = 'mk_adaln_d1_jaxref_r8_ab5333'

def setup_inputs(seed: int=0):
    np.random.seed(seed)
    _w = jnp.asarray

    def _L0_attn_setup():
        import jax, jax.numpy as jnp
        import numpy as np
        D_MODEL = 256
        D_INNER = 512
        D_STATE = 64
        N_QK_HEADS = 8
        N_V_HEADS = 64
        CHUNK = 128
        KSIZE = 4
        CONV_DIM = D_INNER + 2 * N_QK_HEADS * D_STATE
        PROJ_DIM = CONV_DIM + D_INNER + N_V_HEADS

        def segsum(x):
            T = x.shape[-1]
            xe = jnp.broadcast_to(x[..., None], x.shape + (T,))
            strict_lower = jnp.tril(jnp.ones((T, T), dtype=bool), -1)
            xe = jnp.where(strict_lower, xe, 0.0)
            s = jnp.cumsum(xe, axis=-2)
            lower = jnp.tril(jnp.ones((T, T), dtype=bool), 0)
            return jnp.where(lower, s, -jnp.inf)

        def ssd_chunk_scan(X, dA, Bm, Cm, chunk):
            b, l, h, p = X.shape
            g = Bm.shape[2]
            rep = h // g
            Bm = jnp.repeat(Bm, rep, axis=2)
            Cm = jnp.repeat(Cm, rep, axis=2)
            c = l // chunk
            X = X.reshape(b, c, chunk, h, p)
            Bm = Bm.reshape(b, c, chunk, h, -1)
            Cm = Cm.reshape(b, c, chunk, h, -1)
            A = jnp.transpose(dA.reshape(b, c, chunk, h), (0, 3, 1, 2))
            A_cum = jnp.cumsum(A, axis=-1)
            Lm = jnp.exp(segsum(A))
            Y_diag = jnp.einsum('bcshn,bczhn,bhcsz,bczhp->bcshp', Cm, Bm, Lm, X)
            decay_states = jnp.exp(A_cum[..., -1:] - A_cum)
            states = jnp.einsum('bcshn,bhcs,bcshp->bchpn', Bm, decay_states, X)
            states = jnp.concatenate([jnp.zeros_like(states[:, :1]), states], axis=1)
            chunk_sums = jnp.pad(A_cum[..., -1], ((0, 0), (0, 0), (1, 0)))
            decay_chunk = jnp.exp(segsum(chunk_sums))
            new_states = jnp.einsum('bhzc,bchpn->bzhpn', decay_chunk, states)
            states = new_states[:, :-1]
            state_decay_out = jnp.exp(A_cum)
            Y_off = jnp.einsum('bcshn,bchpn,bhcs->bcshp', Cm, states, state_decay_out)
            return (Y_diag + Y_off).reshape(b, l, h, p)
        key = jax.random.key(seed)
        ks = jax.random.split(key, 6)
        input_ = jax.random.normal(ks[0], (2, 512, D_MODEL), dtype=jnp.float32)
        in_proj_w = jax.random.normal(ks[1], (PROJ_DIM, D_MODEL), dtype=jnp.float32) * (2.0 / D_MODEL) ** 0.5
        cb = (CONV_DIM * KSIZE) ** (-0.5)
        conv1d_weight = jax.random.uniform(ks[2], (CONV_DIM, 1, KSIZE), dtype=jnp.float32, minval=-cb, maxval=cb)
        conv1d_bias = jax.random.uniform(ks[3], (CONV_DIM,), dtype=jnp.float32, minval=-0.5, maxval=0.5)
        z_bias = jnp.zeros((D_INNER,), dtype=jnp.float32)
        D = jnp.ones((N_V_HEADS,), dtype=jnp.float32)
        out_proj_w = jax.random.normal(ks[4], (D_MODEL, D_INNER), dtype=jnp.float32) * (2.0 / D_INNER) ** 0.5
        return {'input_': input_, 'in_proj_w': in_proj_w, 'conv1d_weight': conv1d_weight, 'conv1d_bias': conv1d_bias, 'z_bias': z_bias, 'D': D, 'out_proj_w': out_proj_w}
    _L0_attn_in = _L0_attn_setup()

    def _L0_ffn_setup():
        import jax, jax.numpy as jnp
        import numpy as np
        D = 256
        H_TOTAL = 1024
        E = 8
        K = 2
        HE = H_TOTAL // E
        B, S = (2, 256)
        key = jax.random.key(seed)
        ks = jax.random.split(key, 8)
        scale_up = 1.0 / np.sqrt(D)
        scale_dn = 1.0 / np.sqrt(HE)
        return {'x': jax.random.normal(ks[0], (B, S, D), dtype=jnp.float32), 'Wg1': jax.random.normal(ks[1], (E, D), dtype=jnp.float32) * 0.02, 'Wg2': jax.random.normal(ks[2], (E, E), dtype=jnp.float32) * 0.2, 'Wup': jax.random.uniform(ks[3], (E, HE, D), dtype=jnp.float32, minval=-scale_up, maxval=scale_up), 'bup': jax.random.uniform(ks[4], (E, HE), dtype=jnp.float32, minval=-scale_up, maxval=scale_up), 'Wdown': jax.random.uniform(ks[5], (E, D, HE), dtype=jnp.float32, minval=-scale_dn, maxval=scale_dn), 'bdown': jax.random.uniform(ks[6], (E, D), dtype=jnp.float32, minval=-scale_dn, maxval=scale_dn)}
    _L0_ffn_in = _L0_ffn_setup()
    _L0_c = _w((lambda *s: np.random.randn(*s).astype(np.float32) * 0.05)(4, 256))
    _L0_wmod = _w((lambda *s: np.random.randn(*s).astype(np.float32) * 0.05)(256, 6 * 256) * 256 ** (-0.5))
    _d = {'L0_attn_input_': _L0_attn_in['input_'], 'L0_attn_in_proj_w': _L0_attn_in['in_proj_w'], 'L0_attn_conv1d_weight': _L0_attn_in['conv1d_weight'], 'L0_attn_conv1d_bias': _L0_attn_in['conv1d_bias'], 'L0_attn_z_bias': _L0_attn_in['z_bias'], 'L0_attn_D': _L0_attn_in['D'], 'L0_attn_out_proj_w': _L0_attn_in['out_proj_w'], 'L0_ffn_Wg1': _L0_ffn_in['Wg1'], 'L0_ffn_Wg2': _L0_ffn_in['Wg2'], 'L0_ffn_Wup': _L0_ffn_in['Wup'], 'L0_ffn_bup': _L0_ffn_in['bup'], 'L0_ffn_Wdown': _L0_ffn_in['Wdown'], 'L0_ffn_bdown': _L0_ffn_in['bdown'], 'L0_c': _L0_c, 'L0_wmod': _L0_wmod}
    _x0 = _d['L0_attn_input_']
    _d['L0_attn_input_'] = jax.random.normal(jax.random.fold_in(jax.random.key(seed), 1), (4, 512, 256), dtype=_x0.dtype)
    del _x0
    return _d

def reference(L0_attn_input_, L0_attn_in_proj_w, L0_attn_conv1d_weight, L0_attn_conv1d_bias, L0_attn_z_bias, L0_attn_D, L0_attn_out_proj_w, L0_ffn_Wg1, L0_ffn_Wg2, L0_ffn_Wup, L0_ffn_bup, L0_ffn_Wdown, L0_ffn_bdown, L0_c, L0_wmod):

    def _L0_attn_ref(input_, in_proj_w, conv1d_weight, conv1d_bias, z_bias, D, out_proj_w):
        import jax, jax.numpy as jnp
        import numpy as np
        D_MODEL = 256
        D_INNER = 512
        D_STATE = 64
        N_QK_HEADS = 8
        N_V_HEADS = 64
        CHUNK = 128
        KSIZE = 4
        CONV_DIM = D_INNER + 2 * N_QK_HEADS * D_STATE
        PROJ_DIM = CONV_DIM + D_INNER + N_V_HEADS

        def segsum(x):
            T = x.shape[-1]
            xe = jnp.broadcast_to(x[..., None], x.shape + (T,))
            strict_lower = jnp.tril(jnp.ones((T, T), dtype=bool), -1)
            xe = jnp.where(strict_lower, xe, 0.0)
            s = jnp.cumsum(xe, axis=-2)
            lower = jnp.tril(jnp.ones((T, T), dtype=bool), 0)
            return jnp.where(lower, s, -jnp.inf)

        def ssd_chunk_scan(X, dA, Bm, Cm, chunk):
            b, l, h, p = X.shape
            g = Bm.shape[2]
            rep = h // g
            Bm = jnp.repeat(Bm, rep, axis=2)
            Cm = jnp.repeat(Cm, rep, axis=2)
            c = l // chunk
            X = X.reshape(b, c, chunk, h, p)
            Bm = Bm.reshape(b, c, chunk, h, -1)
            Cm = Cm.reshape(b, c, chunk, h, -1)
            A = jnp.transpose(dA.reshape(b, c, chunk, h), (0, 3, 1, 2))
            A_cum = jnp.cumsum(A, axis=-1)
            Lm = jnp.exp(segsum(A))
            Y_diag = jnp.einsum('bcshn,bczhn,bhcsz,bczhp->bcshp', Cm, Bm, Lm, X)
            decay_states = jnp.exp(A_cum[..., -1:] - A_cum)
            states = jnp.einsum('bcshn,bhcs,bcshp->bchpn', Bm, decay_states, X)
            states = jnp.concatenate([jnp.zeros_like(states[:, :1]), states], axis=1)
            chunk_sums = jnp.pad(A_cum[..., -1], ((0, 0), (0, 0), (1, 0)))
            decay_chunk = jnp.exp(segsum(chunk_sums))
            new_states = jnp.einsum('bhzc,bchpn->bzhpn', decay_chunk, states)
            states = new_states[:, :-1]
            state_decay_out = jnp.exp(A_cum)
            Y_off = jnp.einsum('bcshn,bchpn,bhcs->bcshp', Cm, states, state_decay_out)
            return (Y_diag + Y_off).reshape(b, l, h, p)
        b, L, _ = input_.shape
        xBCzA = jnp.einsum('bld,ed->ble', input_, in_proj_w)
        xBC = xBCzA[..., :CONV_DIM]
        z = xBCzA[..., CONV_DIM:CONV_DIM + D_INNER]
        A_log = xBCzA[..., CONV_DIM + D_INNER:]
        xt = jnp.transpose(xBC, (0, 2, 1))
        y = jax.lax.conv_general_dilated(xt, conv1d_weight, (1,), [(KSIZE - 1, 0)], feature_group_count=CONV_DIM, dimension_numbers=('NCH', 'OIH', 'NCH'))
        xBC = jax.nn.silu(jnp.transpose(y + conv1d_bias[None, :, None], (0, 2, 1)))
        x = xBC[..., :D_INNER].reshape(b, L, N_V_HEADS, D_INNER // N_V_HEADS)
        Bm = xBC[..., D_INNER:D_INNER + N_QK_HEADS * D_STATE].reshape(b, L, N_QK_HEADS, D_STATE)
        Cm = xBC[..., D_INNER + N_QK_HEADS * D_STATE:].reshape(b, L, N_QK_HEADS, D_STATE)
        dt = jax.nn.softplus(A_log)
        x_in = x / dt[..., None]
        y_ssm = ssd_chunk_scan(x_in * dt[..., None], -dt, Bm, Cm, CHUNK)
        Du = D[None, None, :, None] * x_in
        yf = (y_ssm + Du).reshape(b, L, D_INNER)
        out = jnp.einsum('bld,ed->ble', yf * jax.nn.silu(z + z_bias), out_proj_w)
        return out

    def _L0_ffn_ref(x, Wg1, Wg2, Wup, bup, Wdown, bdown):
        import jax, jax.numpy as jnp
        import numpy as np
        D = 256
        H_TOTAL = 1024
        E = 8
        K = 2
        HE = H_TOTAL // E
        B, S = (2, 256)
        Bd, Sd, Dd = x.shape
        T = Bd * Sd
        xt = x.reshape(T, Dd)
        logits = jnp.tanh(xt @ Wg1.T) @ Wg2.T
        _, top_idx = jax.lax.top_k(logits, K)
        top_logits = jnp.take_along_axis(logits, top_idx, axis=1)
        top_scores = jax.nn.softmax(top_logits.astype(jnp.float32), axis=1).astype(logits.dtype)
        rows = jnp.arange(T)[:, None]
        scores = jnp.zeros_like(logits).at[rows, top_idx].set(top_scores)
        up = jnp.einsum('td,ehd->teh', xt, Wup) + bup
        h = jax.nn.silu(up)
        down = jnp.einsum('teh,eoh->teo', h, Wdown) + bdown
        out = jnp.einsum('te,teo->to', scores, down)
        return out.reshape(Bd, Sd, Dd)
    x = L0_attn_input_
    mod = (_silu(L0_c) @ L0_wmod).reshape(L0_c.shape[0], 6, 1, -1)
    sa, ca, ga, sb, cb, gb = (mod[:, 0], mod[:, 1], mod[:, 2], mod[:, 3], mod[:, 4], mod[:, 5])
    ga = (2 * (ga >= 0) - 1) * jnp.maximum(jnp.abs(ga), 0.25)
    gb = (2 * (gb >= 0) - 1) * jnp.maximum(jnp.abs(gb), 0.25)
    h = _layernorm(x, axis=-1) * (1 + ca) + sa
    x = x + ga * _L0_attn_ref(h, L0_attn_in_proj_w, L0_attn_conv1d_weight, L0_attn_conv1d_bias, L0_attn_z_bias, L0_attn_D, L0_attn_out_proj_w)
    h = _layernorm(x, axis=-1) * (1 + cb) + sb
    x = x + gb * _L0_ffn_ref(h, L0_ffn_Wg1, L0_ffn_Wg2, L0_ffn_Wup, L0_ffn_bup, L0_ffn_Wdown, L0_ffn_bdown)
    return x

_drawn_inputs = setup_inputs


def setup_inputs(seed=0):
    import zlib

    import numpy as np

    out = dict(_drawn_inputs(seed))
    spreads = {'L0_attn_z_bias': (0.0, 0.342), 'L0_attn_D': (1.0, 0.2)}
    factors = {'L0_ffn_bup': 30.315, 'L0_ffn_bdown': 6.503}
    for name, (base, spread) in spreads.items():
        noise = np.random.default_rng([zlib.crc32(name.encode()), seed]).standard_normal(out[name].shape)
        drawn = base * np.exp(spread * noise) if base else spread * noise
        out[name] = jnp.asarray(drawn.astype(out[name].dtype))
    for name, factor in factors.items():
        out[name] = (out[name] * factor).astype(out[name].dtype)
    return out
```

```python
from contextlib import ExitStack

import concourse.bass as bass
from concourse import mybir

P = 128
BATCH, SEQ, DM = 4, 512, 256
DI, N_HEAD, HEAD, N_GRP, D_STATE = 512, 64, 8, 8, 64
KSIZE = 4
CHUNK = 64
N_EXP, D_EXP = 8, 128
TOK = BATCH * SEQ
N_TILE = TOK // P
TPB = SEQ // P
KD = DM // P
CT_ = DI // P
N_PROJ = 4 * CT_
N_CONV = 3 * CT_
N_IN = 4 * DI + N_HEAD
EPS = 1e-5
RANGE = 60.0
TINY = 1e-30
G_BANK = 2
LEVELS = 8

F32 = mybir.dt.float32
BF16 = mybir.dt.bfloat16
I32 = mybir.dt.int32
ALU = mybir.AluOpType
ACT = mybir.ActivationFunctionType
AX = mybir.AxisListType

C_ID, C_ONE, C_TRI, C_RANK = 0, P, 2 * P, 2 * P + CHUNK
C_ALL = C_RANK + N_EXP * N_EXP
E_MID, E_AB, E_BH, E_AL = 0, P, 2 * P, 3 * P
E_ALL = 4 * P


def program_order():
    steps = [("mod",)]
    steps += [("ln1", b) for b in range(BATCH)]
    steps += [("dt", 0), ("dt", 1)]
    steps += [("softplus",), ("factors", 0), ("factors", 1), ("decays",), ("flag",)]
    steps += [("proj", 0, m) for m in range(N_PROJ)]
    for slot in range(BATCH + 1):
        steps.append(("gates", slot))
        proj = [("proj", slot + 1, m) for m in range(N_PROJ)] if slot + 1 < BATCH else []
        ffn = []
        if slot:
            b = slot - 1
            ffn = [("hid", b), ("gate1", b), ("gate2", b), ("score", b), ("spread", b)]
            ffn += [("up", b, e) for e in range(N_EXP)]
            ffn += [("down", b, i) for i in range(TPB)]
        rest = len(ffn)
        if slot < BATCH:
            for i in range(TPB):
                for n, kind in enumerate(("tr", "state", "y", "z", "out")):
                    steps.append((kind, slot, i))
                    if n < 3 and proj:
                        steps.append(proj.pop(0))
                    if ffn and n < 4:
                        steps.append(ffn.pop(0))
                    if kind == "out":
                        steps.append(("norm", slot, i))
        steps += ffn
        steps += proj
    return steps


def bank_jobs(step, tail):
    kind = step[0]
    ffn = [7, 2, 0, 1, 5, 6] if tail else [7, 2]
    if kind == "mod":
        return {"mod": 7}
    if kind == "ln1":
        return {("hT", step[1], k): (0, 1, 2, 3)[2 * (step[1] % 2) + k] for k in range(KD)}
    if kind == "dt":
        return {("dt", step[1]): 5 + step[1]}
    if kind == "factors":
        return {("E", step[1]): step[1]}
    if kind == "decays":
        return {("D", n): (2, 3, 4, 5)[n] for n in range(4)}
    if kind == "flag":
        return {"flag": 7}
    if kind == "proj":
        return {step: step[2] % 2}
    if kind == "gates":
        return {step: 7}
    if kind == "tr":
        return {("xt",) + step[1:]: 2, ("bt",) + step[1:]: 2,
                ("cb", 0) + step[1:]: 3, ("cb", 1) + step[1:]: 4}
    if kind == "state":
        jobs = {("st", 0) + step[1:]: 3, ("st", 1) + step[1:]: 4}
        if step[2] == TPB - 1:
            del jobs[("st", 1) + step[1:]]
        return jobs
    if kind == "y":
        return {("y", 0) + step[1:]: 5, ("y", 1) + step[1:]: 6}
    if kind == "z":
        return {step: 2}
    if kind == "out":
        return {step: 7}
    if kind == "hid":
        return {("hid", step[1], 0): 7, ("hid", step[1], 1): 2}
    if kind in ("gate1", "gate2"):
        return {step: 7}
    if kind == "spread":
        return {("sT", step[1]): 7, ("s3", step[1]): 2}
    if kind == "up":
        e = step[2]
        return {step: ffn[2 * e % len(ffn)], ("bc",) + step[1:]: ffn[(2 * e + 1) % len(ffn)]}
    if kind == "down":
        return {step: ffn[(3 + step[2]) % len(ffn)]}
    return {}


def adaln_block(nc, x_d, cT_d, wmod_d, win_d, cw_d, cb_d, zb_d, dh_d, wo_d, wg1_d, wg2_d,
                wup_d, bup_d, wdn_d, bdn_d, const_d, early_d, sel_d, gen_d, out_d):
    STEPS = program_order()
    tail_from = max(n for n, s in enumerate(STEPS) if s[0] in ("out", "norm"))
    bank_of, use_no, used = {}, {}, [0] * 8
    for n, step in enumerate(STEPS):
        for job, bank in bank_jobs(step, n > tail_from).items():
            bank_of[job], use_no[job] = bank, used[bank]
            used[bank] += 1
    g_after = {}
    for n, step in enumerate(STEPS):
        for job, bank in bank_jobs(step, n > tail_from).items():
            if bank == G_BANK:
                last_job = job
        if step[0] == "y":
            g_after[step[1:]] = last_job

    with ExitStack() as ctx:
        def sb(name, shape, dt=F32):
            return ctx.enter_context(nc.sbuf_tensor(name, shape, dt))

        def sem(name):
            return ctx.enter_context(nc.semaphore(name))

        ps = ctx.enter_context(nc.psum_tensor("ps", [P, 8, 512], F32))

        cst = sb("cst", [P, C_ALL])
        win = sb("win", [P, KD, N_IN])
        cw = sb("cw", [P, N_CONV, KSIZE])
        cb = sb("cb", [P, N_CONV])
        zb = sb("zb", [P, CT_])
        dh = sb("dh", [P, N_HEAD])
        wog = sb("wog", [P, CT_, DM])
        wg1 = sb("wg1", [P, KD, N_EXP])
        wg2 = sb("wg2", [N_EXP, N_EXP])
        wup = sb("wup", [P, KD, N_EXP * D_EXP])
        bup = sb("bup", [P, N_EXP])
        wdg = sb("wdg", [P, N_EXP, DM])
        bdg = sb("bdg", [N_EXP, DM])
        sel = sb("sel", [3 * N_EXP, N_EXP, P], BF16)
        identb = sb("identb", [P, P], BF16)
        half = sb("half", [P, 1])
        csb = sb("csb", [P, KD, BATCH])
        csil = sb("csil", [P, KD, BATCH])
        modT = sb("modT", [P, 6 * KD, BATCH])
        gates = sb("gates", [P, 2, DM])
        gsg = sb("gsg", [P, 2, KD, BATCH])
        hT = sb("hT", [P, KD, TOK])
        x1 = sb("x1", [P, 2, TPB, DM])
        conv = sb("conv", [P, 2, N_CONV, SEQ])
        sz = sb("sz", [P, CT_, SEQ])
        dt = sb("dt", [P, N_TILE, N_HEAD])
        fu = sb("fu", [P, N_TILE, N_HEAD])
        fv = sb("fv", [P, N_TILE, N_HEAD])
        fq = sb("fq", [P, N_TILE, N_HEAD])
        dec = sb("dec", [P, N_TILE, 2, N_HEAD // 2])
        flg = sb("flg", [P, 2])
        flsum = sb("flsum", [P, 1])
        flag = sb("flag", [1, 1], I32)
        xtok = sb("xtok", [P, 2, DI])
        xv = sb("xv", [P, 2, DI])
        btok = sb("btok", [P, 2, DI])
        gm = sb("gm", [P, 2, 2, 4 * CHUNK])
        ytok = sb("ytok", [P, 2, DI])
        yT = sb("yT", [P, 2, CT_, P])
        st = sb("st", [P, 4, 4 * CHUNK])
        scr = sb("scr", [P, 2, KD * P])
        xn = sb("xn", [P, 4, DM])
        bns = sb("bns", [P, 2, 6])
        mv = sb("mv", [P, 2, 2])
        rst = sb("rst", [P, 2, 1])
        hs = sb("hs", [P, N_EXP, SEQ])
        lg = sb("lg", [P, TPB, N_EXP])
        top = sb("top", [P, TPB, N_EXP])
        cmp_ = sb("cmp", [P, TPB, N_EXP, N_EXP])
        eq = sb("eq", [P, TPB, N_EXP, N_EXP])
        rank = sb("rank", [P, TPB, N_EXP])
        msum = sb("msum", [P, TPB])
        dl = sb("dl", [P, TPB, N_EXP])
        tl = sb("tl", [P, TPB, N_EXP])
        sc = sb("sc", [P, TPB, N_EXP])
        s3 = sb("s3", [P, TPB, 3, N_EXP], BF16)
        sT = sb("sT", [N_EXP, SEQ])
        th = sT
        s3T = sb("s3T", [3 * N_EXP, SEQ], BF16)
        g_tab = sb("g_tab", [P, 3, P])
        g_fac = sb("g_fac", [P, 2, N_HEAD])
        g_xs = sb("g_xs", [P, DI])
        g_st = sb("g_st", [P, 4 * CHUNK])
        g_dec = sb("g_dec", [P, N_HEAD // 2])
        lent = conv[:, 1].rearrange("p m t -> p (m t)")
        xin = lent[:, 0:N_TILE * DM].rearrange("p (i d) -> p i d", i=N_TILE)
        half_cols = (N_TILE // 2) * N_HEAD
        base = N_TILE * DM
        sp_t, sp_l = (lent[:, base + 1024 * k:base + 1024 * (k + 1)] for k in range(2))
        sp_w = xtok[:, :, :].rearrange("p a c -> p (a c)")
        sp_m = ytok[:, :, :].rearrange("p a c -> p (a c)")
        early = yT[:, 0].rearrange("p m t -> p (m t)")
        sel32 = xv[0:3 * N_EXP, :, :].rearrange("p a c -> p (a c)")
        wmod = hs[:, :, :].rearrange("p e t -> p (e t)")[:, 0:KD * 6 * DM].rearrange("p (k n) -> p k n", k=KD)
        dt_f = dt[:, :, :].rearrange("p i h -> p (i h)")
        fu_f = fu[:, :, :].rearrange("p i h -> p (i h)")
        fv_f = fv[:, :, :].rearrange("p i h -> p (i h)")
        fq_f = fq[:, :, :].rearrange("p i h -> p (i h)")
        ident = cst[:, C_ID:C_ID + P]

        ld_x = [sem(f"ld_x{b}") for b in range(BATCH)]
        names = ["cst", "c", "wmod", "win", "small", "wup", "ffn"]
        ld = {n: sem("ld_" + n) for n in names}
        ld_wo = sem("ld_wo")
        ld_wd = sem("ld_wd")
        ld_bd = sem("ld_bd")
        ld_res = [sem(f"ld_res{k}") for k in range(2)]
        full = [sem(f"bank{k}_full") for k in range(8)]
        consts_made = sem("consts_made")
        consts_cast = sem("consts_cast")
        csil_ready = sem("csil_ready")
        mod_ready = sem("mod_ready")
        diag_ready = sem("diag_ready")
        gates_ready = sem("gates_ready")
        pool_chain = sem("pool_chain")
        dve_chain = sem("dve_chain")
        act_chain = sem("act_chain")
        var_ready = sem("var_ready")
        rstd_ready = sem("rstd_ready")
        xn_ready = sem("xn_ready")
        xn_used = sem("xn_used")
        hT_ready = sem("hT_ready")
        abs_ready = sem("abs_ready")
        relu_ready = sem("relu_ready")
        expt_ready = sem("expt_ready")
        onep_ready = sem("onep_ready")
        ln_ready = sem("ln_ready")
        dt_ready = sem("dt_ready")
        q_ready = sem("q_ready")
        eclip_ready = sem("eclip_ready")
        uv_ready = sem("uv_ready")
        dec_ready = sem("dec_ready")
        clip_counted = sem("clip_counted")
        flag_ready = sem("flag_ready")
        tap0 = sem("tap0_written")
        taps = sem("taps_added")
        silu_done = sem("silu_done")
        xtok_ready = sem("xtok_ready")
        btok_ready = sem("btok_ready")
        gm_ready = sem("gm_ready")
        xv_ready = sem("xv_ready")
        xq_ready = sem("xq_ready")
        st_ready = sem("st_ready")
        yo_done = sem("yo_done")
        lg_ready = sem("lg_ready")
        ytok_ready = sem("ytok_ready")
        yT_ready = sem("yT_ready")
        x1_ready = sem("x1_ready")
        wog_ready = sem("wog_ready")
        wdg_ready = sem("wdg_ready")
        hid_ready = sem("hid_ready")
        th_ready = sem("th_ready")
        dl_ready = sem("dl_ready")
        tl_ready = sem("tl_ready")
        sc_ready = sem("sc_ready")
        sT_ready = sem("sT_ready")
        h_ready = sem("h_ready")
        hs_ready = sem("hs_ready")
        x2_ready = sem("x2_ready")
        g_table = sem("general_table_loaded")
        g_pe = sem("general_tensor_steps")
        g_act = sem("general_scalar_steps")
        g_dve = sem("general_vector_steps")
        stored = [sem(f"stored{k}") for k in range(2)]

        def bank(job):
            return ps[:, bank_of[job], :]

        def wait_bank(eng, job):
            eng.wait_ge(full[bank_of[job]], use_no[job] + 1)

        def done(eng, kind, tiles):
            if tiles > 0:
                where = divmod(tiles - 1, TPB)
                wait_bank(eng, (kind, 1) + where if kind == "y" else (kind,) + where)

        def tile_no(b, i):
            return b * TPB + i

        def chunks_before(b, i):
            return b * (2 * TPB - 1) + 2 * i

        def releases():
            when = {"mod": (mod_ready, 1), "flag": (flag_ready, 1)}
            for b in range(BATCH):
                for k in range(KD):
                    when["hT", b, k] = (hT_ready, KD * b + k + 1)
                    when["hid", b, k] = (hid_ready, KD * b + k + 1)
                for m in range(N_PROJ):
                    when["proj", b, m] = ((taps, 3 * (N_CONV * b + m + 1)) if m < N_CONV
                                          else (silu_done, N_PROJ * b + m + 1))
                when["gate1", b] = (th_ready, b + 1)
                when["gate2", b] = (lg_ready, b + 1)
                when["sT", b] = (sT_ready, 2 * b + 1)
                when["s3", b] = (sT_ready, 2 * b + 2)
                for e in range(N_EXP):
                    when["up", b, e] = (h_ready, N_EXP * b + e + 1)
                    when["bc", b, e] = (hs_ready, N_EXP * b + e + 1)
                for i in range(TPB):
                    n = tile_no(b, i)
                    when["xt", b, i] = (xtok_ready, n + 1)
                    when["bt", b, i] = (btok_ready, n + 1)
                    when["z", b, i] = (yT_ready, n + 1)
                    when["out", b, i] = (x1_ready, n + 1)
                    when["down", b, i] = (x2_ready, n + 1)
                    for a in range(2):
                        when["cb", a, b, i] = (gm_ready, 2 * n + a + 1)
                        when["st", a, b, i] = (st_ready, chunks_before(b, i) + a + 1)
                        when["y", a, b, i] = (ytok_ready, 2 * n + a + 1)
            for b in range(BATCH + 1):
                when["gates", b] = (gates_ready, b + 1)
            for h in range(2):
                when["dt", h] = (relu_ready, h + 1)
                when["E", h] = (clip_counted, h + 1)
            for n in range(4):
                when["D", n] = (dec_ready, 2 * n + 2)
            return when

        when_read = releases()
        before = {}
        for job in bank_of:
            for other in bank_of:
                if bank_of[other] == bank_of[job] and use_no[other] == use_no[job] - 1:
                    before[job] = other

        def wait_bank_free(pe, job):
            if job in before:
                pe.wait_ge(*when_read[before[job]])

        G_PRE = {"pe": 1, "act": 0, "dve": 2}
        G_LEVEL = {"pe": 5, "act": 1, "dve": 7}
        G_FIRST = {"pe": 2, "act": 3, "dve": 2}
        G_OTHER = {"pe": 4, "act": 3, "dve": 7}

        def g_before(engine, n):
            rows, i = divmod(n, TPB)
            tiles_first = rows + (1 if i else 0)
            return (n * (G_PRE[engine] + LEVELS * G_LEVEL[engine]) + tiles_first * G_FIRST[engine]
                    + (n - tiles_first) * G_OTHER[engine])

        g_bank = ps[:, G_BANK, :]

        def general_pe(pe, b, i):
            n = tile_no(b, i)
            p0, a0, d0 = (g_before(e, n) for e in ("pe", "act", "dve"))
            tok = slice(i * P, (i + 1) * P)
            pe.wait_ge(*when_read[g_after[b, i]])
            for j in range(CT_):
                ins = pe.transpose(g_bank[:, j * P:(j + 1) * P], conv[:, b % 2, j, tok], ident)
            ins.then_inc(g_pe, 1)
            p, a, d = p0 + G_PRE["pe"], a0 + G_PRE["act"], d0 + G_PRE["dve"]
            with pe.Fori(0, LEVELS) as lv:
                pe.wait_ge(g_dve, d + lv * G_LEVEL["dve"])
                pe.wait_ge(g_table, 16 * ((LEVELS + 1) * n + 1) + 16 * lv)
                for w in range(2):
                    ins = pe.matmul(g_bank[:, w * N_HEAD:(w + 1) * N_HEAD], g_tab[:, w, :], dt[:, n, :],
                                    start=True, stop=True)
                ins.then_inc(g_pe, 1)
                pe.wait_ge(g_act, a + 1 + lv * G_LEVEL["act"])
                for par in range(2):
                    if par:
                        pe.wait_ge(g_dve, d + 4 + lv * G_LEVEL["dve"])
                    rows = slice(64 * par, 64 * par + 64)
                    for j in range(CT_):
                        ins = pe.matmul(g_bank[:, j * P:(j + 1) * P], conv[rows, b % 2, CT_ + j, tok],
                                        conv[rows, b % 2, 2 * CT_ + j, tok], start=True, stop=True)
                    ins.then_inc(g_pe, 1)
                    pe.wait_ge(g_dve, d + 2 + 3 * par + lv * G_LEVEL["dve"])
                    for j in range(CT_):
                        g = 2 * j + par
                        ins = pe.matmul(g_bank[:, j * 64:(j + 1) * 64], g_gm(n)[:, j * P:(j + 1) * P],
                                        g_xs[:, g * 64:(g + 1) * 64], start=True, stop=True)
                    ins.then_inc(g_pe, 1)
            p, a, d = (p + LEVELS * G_LEVEL["pe"], a + LEVELS * G_LEVEL["act"], d + LEVELS * G_LEVEL["dve"])
            pe.wait_ge(g_dve, d)
            pe.wait_ge(g_table, 16 * (LEVELS + 1) * (n + 1))
            for w in range(3):
                ins = pe.matmul(g_bank[:, w * N_HEAD:(w + 1) * N_HEAD], g_tab[:, w, :], dt[:, n, :],
                                start=True, stop=True)
            ins.then_inc(g_pe, 1)
            pe.wait_ge(g_act, a + 3)
            pe.wait_ge(g_dve, d + 1)
            if i:
                for par in range(2):
                    if par:
                        pe.wait_ge(g_dve, d + 3)
                    rows = slice(64 * par, 64 * par + 64)
                    for j in range(CT_):
                        ins = pe.matmul(g_bank[:, j * 64:(j + 1) * 64], conv[rows, b % 2, 2 * CT_ + j, tok],
                                        g_st[rows, j * 64:(j + 1) * 64], start=True, stop=True)
                    ins.then_inc(g_pe, 1)
                pe.wait_ge(g_dve, d + 5)
            for g in range(N_GRP):
                j, par = g // 2, g % 2
                ins = pe.matmul(ps[64 * par:64 * par + 64, G_BANK, j * 64:(j + 1) * 64],
                                btok[:, n % 2, g * 64:(g + 1) * 64], g_xs[:, g * 64:(g + 1) * 64],
                                start=True, stop=True)
            ins.then_inc(g_pe, 1)
            pe.wait_ge(g_dve, g_before("dve", n + 1))

        def general_act(act, b, i):
            n = tile_no(b, i)
            p0, a0, d0 = (g_before(e, n) for e in ("pe", "act", "dve"))
            p, d = p0 + G_PRE["pe"], d0 + G_PRE["dve"]
            with act.Fori(0, LEVELS) as lv:
                act.wait_ge(g_dve, d + lv * G_LEVEL["dve"])
                act.dma_start(g_tab[:, :, :], g_src[bass.ds(lv, 1)].rearrange("o p w c -> (o p) w c")
                              ).then_inc(g_table, 16)
                act.wait_ge(g_pe, p + 1 + lv * G_LEVEL["pe"])
                act.activation(g_fac[:, :, :].rearrange("p w h -> p (w h)"), g_bank[:, 0:2 * N_HEAD], ACT.Exp,
                               scale=-1.0).then_inc(g_act, 1)
            p, d = p + LEVELS * G_LEVEL["pe"], d + LEVELS * G_LEVEL["dve"]
            act.wait_ge(g_dve, d)
            act.dma_start(g_tab[:, :, :], g_src[LEVELS]).then_inc(g_table, 16)
            act.wait_ge(g_pe, p + 1)
            act.activation(g_fac[:, :, :].rearrange("p w h -> p (w h)"), g_bank[:, 0:2 * N_HEAD], ACT.Exp,
                           scale=-1.0).then_inc(g_act, 1)
            for par in range(2):
                rows = slice(64 * par, 64 * par + 64)
                src = ps[rows, G_BANK, 2 * N_HEAD:3 * N_HEAD].rearrange("p (j a h) -> p a j h", a=2, h=8)[:, par]
                act.activation(g_dec[rows, :].rearrange("p (j h) -> p j h", h=8), src, ACT.Exp,
                               scale=-1.0).then_inc(g_act, 1)
            act.preload_act_table(ACT.Silu)
            act.wait_ge(g_dve, g_before("dve", n + 1))

        def general_dve(dve, b, i):
            n = tile_no(b, i)
            p0, a0, d0 = (g_before(e, n) for e in ("pe", "act", "dve"))
            xraw = xv[:, n % 2, :]
            y = ytok[:, n % 2, :]

            def scaled(w):
                return g_fac[:, w, :, None].to_broadcast([P, N_HEAD, HEAD])

            def add_y(par, count):
                yv = y.rearrange("p (j a h d) -> p a j h d", a=2, h=8, d=HEAD)[:, par]
                u = g_fac[:, 1, :].rearrange("p (j a h) -> p a j h", a=2, h=8)[:, par]
                part = scr[:, 0, :].rearrange("p (j h d) -> p j h d", h=8, d=HEAD)
                dve.tensor_tensor(part, g_bank[:, 0:256].rearrange("p (j h d) -> p j h d", h=8, d=HEAD),
                                  u[:, :, :, None].to_broadcast([P, CT_, 8, HEAD]), ALU.mult).then_inc(g_dve, 1)
                dve.wait_ge(g_dve, count + 1)
                y3 = y.rearrange("p (j a c) -> p a j c", a=2, c=64)[:, par]
                dve.tensor_tensor(y3, y3, scr[:, 0, :].rearrange("p (j c) -> p j c", c=64),
                                  ALU.add).then_inc(g_dve, 1)

            dve.wait_ge(ytok_ready, 2 * n + 2)
            dve.wait_ge(g_pe, p0 + 1)
            dve.tensor_copy(xraw, g_bank).then_inc(g_dve, 1)
            dve.memset(y, 0.0).then_inc(g_dve, 1)
            p, a, d = p0 + G_PRE["pe"], a0 + G_PRE["act"], d0 + G_PRE["dve"]
            dve.wait_ge(g_dve, d)
            with dve.Fori(0, LEVELS) as lv:
                ld_, lp = lv * G_LEVEL["dve"], lv * G_LEVEL["pe"]
                dve.wait_ge(g_dve, d + ld_)
                dve.wait_ge(g_act, a + 1 + lv * G_LEVEL["act"])
                dve.tensor_tensor(g_xs[:, :].rearrange("p (h d) -> p h d", d=HEAD),
                                  xraw.rearrange("p (h d) -> p h d", d=HEAD), scaled(0),
                                  ALU.mult).then_inc(g_dve, 1)
                for par in range(2):
                    dve.wait_ge(g_pe, p + 2 + 2 * par + lp)
                    dve.tensor_tensor(g_gm(n).rearrange("p (j s) -> p j s", s=P),
                                      g_bank.rearrange("p (j s) -> p j s", s=P),
                                      g_tab[:, 2:3, :].to_broadcast([P, CT_, P]), ALU.mult).then_inc(g_dve, 1)
                    dve.wait_ge(g_pe, p + 3 + 2 * par + lp)
                    add_y(par, d + 2 + 3 * par + ld_)
            p, a, d = (p + LEVELS * G_LEVEL["pe"], a + LEVELS * G_LEVEL["act"], d + LEVELS * G_LEVEL["dve"])
            dve.wait_ge(g_act, a + 3)
            dve.wait_ge(g_dve, d)
            dve.tensor_tensor(g_xs[:, :].rearrange("p (h d) -> p h d", d=HEAD),
                              xraw.rearrange("p (h d) -> p h d", d=HEAD), scaled(0), ALU.mult).then_inc(g_dve, 1)
            if i:
                for par in range(2):
                    dve.wait_ge(g_pe, p + 2 + par)
                    add_y(par, d + 1 + 2 * par)
                dve.wait_ge(g_pe, p + 4)
                s3v = g_st[:, :].rearrange("p (h d) -> p h d", d=HEAD)
                dve.tensor_tensor(s3v, s3v, g_dec[:, :, None].to_broadcast([P, N_HEAD // 2, HEAD]),
                                  ALU.mult).then_inc(g_dve, 1)
                dve.wait_ge(g_dve, d + 6)
                dve.tensor_tensor(g_st[:, :], g_st[:, :], g_bank[:, 0:256], ALU.add).then_inc(g_dve, 1)
            else:
                dve.wait_ge(g_pe, p + 2)
                dve.tensor_copy(g_st[:, :], g_bank[:, 0:256]).then_inc(g_dve, 1)
            dve.wait_ge(g_dve, g_before("dve", n + 1))

        def g_gm(n):
            return gm[:, n % 2].rearrange("p a c -> p (a c)")

        g_src = gen_d.rearrange("l p (w c) -> l p w c", w=3)

        block = ctx.enter_context(nc.Block())

        @block.sync
        def _(sp):
            xr = x_d.rearrange("b (i p) d -> b p i d", p=P)
            outr = out_d.rearrange("b (i p) d -> b p i d", p=P)
            sp.dma_start(xin[:, 0:TPB, :], xr[0]).then_inc(ld_x[0], 16)
            sp.dma_start(cst[:, :], const_d).then_inc(ld["cst"], 16)
            sp.dma_start(early, early_d).then_inc(ld["cst"], 16)
            sp.dma_start(sel32, sel_d).then_inc(ld["cst"], 16)
            sp.dma_start(csb[:, :, :], cT_d.rearrange("(k p) b -> p k b", p=P)).then_inc(ld["c"], 16)
            for b in range(1, BATCH):
                sp.dma_start(xin[:, b * TPB:(b + 1) * TPB, :], xr[b]).then_inc(ld_x[b], 16)
            wmod_r = wmod_d.rearrange("(k p) n -> p k n", p=P)
            sp.dma_start(wmod, wmod_r).then_inc(ld["wmod"], 16)
            sp.dma_start(win[:, :, :], win_d.rearrange("(k p) n -> p k n", p=P)).then_inc(ld["win"], 16)
            for t, d in ((cw[:, :, :], cw_d), (cb[:, :], cb_d), (zb[:, :], zb_d), (dh[:, :], dh_d)):
                sp.dma_start(t, d).then_inc(ld["small"], 16)
            for t, d in ((wg1[:, :, :], wg1_d.rearrange("(k p) e -> p k e", p=P)), (wg2[:, :], wg2_d),
                         (bup[:, :], bup_d)):
                sp.dma_start(t, d).then_inc(ld["ffn"], 16)
            sp.dma_start(wup[:, :, :], wup_d.rearrange("(k p) n -> p k n", p=P)).then_inc(ld["wup"], 16)
            wo_r = wo_d.rearrange("(j p) n -> p j n", p=P)
            wd_r = wdn_d.rearrange("e p n -> p e n")
            for b in range(BATCH + 1):
                if b < BATCH:
                    if b >= 1:
                        done(sp, "out", TPB * b)
                    sp.dma_start(wog[:, :, :], wo_r).then_inc(ld_wo, 16)
                    if b >= 2:
                        sp.wait_ge(stored[b % 2], 16 * TPB * (b // 2))
                    sp.dma_start(x1[:, b % 2], xr[b]).then_inc(ld_res[b % 2], 16)
                    if b >= 1:
                        done(sp, "down", TPB * b)
                    sp.dma_start(wdg[:, :, :], wd_r).then_inc(ld_wd, 16)
                    sp.dma_start(bdg[:, :], bdn_d).then_inc(ld_bd, 16)
                if b >= 1:
                    for i in range(TPB):
                        sp.wait_ge(x2_ready, tile_no(b - 1, i) + 1)
                        sp.dma_start(outr[b - 1][:, i, :], x1[:, (b - 1) % 2, i, :]).then_inc(
                            stored[(b - 1) % 2], 16)
            for k in range(2):
                sp.wait_ge(stored[k], 16 * TPB * (BATCH // 2))

        @block.gpsimd
        def _(pool):
            chain = [0]

            def link(ins):
                chain[0] += 1
                ins.then_inc(pool_chain, 1)
                pool.wait_ge(pool_chain, chain[0])

            def rstd(n):
                pool.wait_ge(var_ready, n + 1)
                link(pool.tensor_scalar(rst[:, n % 2], mv[:, n % 2, 1:2], EPS, None, ALU.add))
                pool.tensor_tensor(rst[:, n % 2], rst[:, n % 2], half[:, 0:1], ALU.pow).then_inc(rstd_ready, 1)

            pool.memset(half[:, :], -0.5).then_inc(consts_made, 1)
            pool.wait_ge(consts_made, 1)
            for step in STEPS:
                kind = step[0]
                if kind == "ln1":
                    for i in range(TPB):
                        rstd(tile_no(step[1], i))
                elif kind == "tr":
                    b, i = step[1:]
                    n = tile_no(b, i)
                    if i == 0:
                        pool.wait_ge(gates_ready, b + 1)
                        pool.wait_ge(ld_wo, 16 * (b + 1))
                        pool.tensor_tensor(wog[:, :, :], wog[:, :, :],
                                           gates[:, 0:1, :].to_broadcast([P, CT_, DM]),
                                           ALU.mult).then_inc(wog_ready, 1)
                    r = n % 2
                    pool.wait_ge(uv_ready, 4)
                    pool.wait_ge(q_ready, 2)
                    pool.wait_ge(xtok_ready, n + 1)
                    if n == 0:
                        pool.wait_ge(consts_cast, 1)
                    if n >= 2:
                        done(pool, "y", n - 1)
                    xh = xtok[:, r].rearrange("p (h d) -> p h d", d=HEAD)
                    pool.tensor_tensor(xv[:, r].rearrange("p (h d) -> p h d", d=HEAD), xh,
                                       fv[:, n, :, None].to_broadcast([P, N_HEAD, HEAD]),
                                       ALU.mult).then_inc(xv_ready, 1)
                    pool.wait_ge(xv_ready, n + 1)
                    pool.tensor_tensor(xh, xh, fq[:, n, :, None].to_broadcast([P, N_HEAD, HEAD]),
                                       ALU.mult).then_inc(xq_ready, 1)
                elif kind == "norm":
                    rstd(N_TILE + tile_no(*step[1:]))
                elif kind == "hid":
                    b = step[1]
                    pool.wait_ge(ld_wd, 16 * (b + 1))
                    pool.wait_ge(ld_bd, 16 * (b + 1))
                    pool.wait_ge(gates_ready, b + 2)
                    pool.tensor_tensor(wdg[:, :, :], wdg[:, :, :],
                                       gates[:, 1:2, :].to_broadcast([P, N_EXP, DM]),
                                       ALU.mult).then_inc(wdg_ready, 1)
                    pool.tensor_tensor(bdg[:, :], bdg[:, :], gates[0:N_EXP, 1, :],
                                       ALU.mult).then_inc(wdg_ready, 1)

        @block.scalar
        def _(act):
            pending = []

            def silu_conv():
                if not pending:
                    return
                b, m = pending.pop()
                act.wait_ge(taps, 3 * (N_CONV * b + m + 1))
                dst = conv[:, b % 2, m, :]
                act.activation(dst, dst, ACT.Silu).then_inc(silu_done, 1)

            out_of_range = [None]
            act.wait_ge(ld["c"], 16)
            act.activation(csil[:, :, :], csb[:, :, :], ACT.Silu).then_inc(csil_ready, 1)
            for step in STEPS:
                kind = step[0]
                if kind == "ln1":
                    b = step[1]
                    act.wait_ge(mod_ready, 3)
                    for k in range(KD):
                        wait_bank(act, ("hT", b, k))
                        act.activation(hT[:, k, b * SEQ:(b + 1) * SEQ], bank(("hT", b, k)), ACT.Identity,
                                       bias=modT[:, k, b:b + 1],
                                       scale=modT[:, KD + k, b:b + 1]).then_inc(hT_ready, 1)
                elif kind == "softplus":
                    for h in range(2):
                        s = slice(512 * h, 512 * h + 512)
                        wait_bank(act, ("dt", h))
                        act.activation(sp_t[:, s], bank(("dt", h)), ACT.Abs).then_inc(abs_ready, 1)
                    for h in range(2):
                        s = slice(512 * h, 512 * h + 512)
                        act.wait_ge(abs_ready, h + 1)
                        act.activation(sp_t[:, s], sp_t[:, s], ACT.Exp, scale=-1.0).then_inc(expt_ready, 1)
                    for h in range(2):
                        s = slice(512 * h, 512 * h + 512)
                        act.wait_ge(onep_ready, h + 1)
                        act.activation(sp_l[:, s], sp_w[:, s], ACT.Ln).then_inc(ln_ready, 1)
                elif kind == "factors":
                    h = step[1]
                    s = slice(512 * h, 512 * h + 512)
                    act.wait_ge(eclip_ready, h + 1)
                    act.activation(fu_f[:, s], sp_l[:, s], ACT.Exp, scale=-1.0).then_inc(uv_ready, 1)
                    act.activation(fv_f[:, s], sp_l[:, s], ACT.Exp).then_inc(uv_ready, 1)
                elif kind == "flag":
                    act.wait_ge(flag_ready, 1)
                    out_of_range[0] = act.value_load(flag[0:1, 0:1])
                elif kind == "decays":
                    for n in range(4):
                        which, h = n // 2, n % 2
                        wait_bank(act, ("D", n))
                        cnt = 8 if n < 3 else 7
                        for par in range(2):
                            rows = slice(64 * par, 64 * par + 64)
                            src = ps[rows, bank_of[("D", n)], 0:cnt * N_HEAD].rearrange(
                                "p (i j a h) -> p i j a h", j=CT_, a=2, h=8)[:, :, :, par, :]
                            dst = dec[rows, 8 * h:8 * h + cnt, which, :].rearrange("p i (j h) -> p i j h", h=8)
                            ins = act.activation(dst, src, ACT.Exp, scale=-1.0)
                            ins.then_inc(dec_ready, 1)
                elif kind == "proj":
                    b, m = step[1:]
                    wait_bank(act, step)
                    if m == 0:
                        act.wait_ge(ld["small"], 64)
                        act.wait_ge(ld["ffn"], 48)
                        if b >= 2:
                            done(act, "y", TPB * (b - 1))
                        if b == 1:
                            act.wait_ge(xn_ready, N_TILE)
                            act.wait_ge(clip_counted, 2)
                            act.wait_ge(uv_ready, 4)
                            act.wait_ge(uv_ready, 4)
                            act.wait_ge(consts_cast, 2)
                            act.wait_ge(dec_ready, 8)
                    if m < N_CONV:
                        act.activation(conv[:, b % 2, m, :], bank(step), ACT.Identity, bias=cb[:, m:m + 1],
                                       scale=cw[:, m, KSIZE - 1:KSIZE]).then_inc(tap0, 1)
                        silu_conv()
                        pending.append((b, m))
                    else:
                        silu_conv()
                        if m == N_CONV:
                            act.wait_ge(yT_ready, TPB * b)
                        act.activation(sz[:, m - N_CONV, :], bank(step), ACT.Silu,
                                       bias=zb[:, m - N_CONV:m - N_CONV + 1]).then_inc(silu_done, 1)
                elif kind == "gates":
                    b = step[1]
                    wait_bank(act, step)
                    act.wait_ge(wog_ready, b)
                    if b >= 2:
                        act.wait_ge(wdg_ready, 2 * (b - 1))
                    lo, hi = (DM if b == BATCH else 0), (DM if b == 0 else 2 * DM)
                    act.activation(gates[:, :, :].rearrange("p a d -> p (a d)")[:, lo:hi], bank(step)[:, lo:hi],
                                   ACT.Copy).then_inc(gates_ready, 1)
                elif kind == "tr":
                    b, i = step[1:]
                    n = tile_no(b, i)
                    wait_bank(act, ("xt", b, i))
                    if n == 0:
                        act.wait_ge(clip_counted, 2)
                    if n >= 2:
                        done(act, "z", n - 1)
                    act.activation(xtok[:, n % 2, :], bank(("xt", b, i)), ACT.Copy).then_inc(xtok_ready, 1)
                    wait_bank(act, ("bt", b, i))
                    if n >= 2:
                        done(act, "y", n - 1)
                    act.activation(btok[:, n % 2, :], bank(("bt", b, i)), ACT.Copy).then_inc(btok_ready, 1)
                elif kind == "y":
                    with act.If(out_of_range[0] > 0):
                        general_act(act, *step[1:])
                elif kind == "hid":
                    b = step[1]
                    for k in range(KD):
                        wait_bank(act, ("hid", b, k))
                        act.activation(hT[:, k, b * SEQ:(b + 1) * SEQ], bank(("hid", b, k)), ACT.Identity,
                                       bias=modT[:, 3 * KD + k, b:b + 1],
                                       scale=modT[:, 4 * KD + k, b:b + 1]).then_inc(hid_ready, 1)
                elif kind == "gate1":
                    wait_bank(act, step)
                    done(act, "down", TPB * step[1])
                    act.activation(th[:, :], bank(step)[0:N_EXP, :], ACT.Tanh).then_inc(th_ready, 1)
                elif kind == "score":
                    b = step[1]
                    act.wait_ge(dl_ready, b + 1)
                    act.activation(tl[:, :, :], dl[:, :, :], ACT.Tanh, scale=0.5).then_inc(tl_ready, 1)
                elif kind == "spread":
                    b = step[1]
                    if b >= 1:
                        done(act, "down", TPB * b)
                    act.wait_ge(lg_ready, b + 1)
                    wait_bank(act, ("sT", b))
                    act.activation(sT[:, :], bank(("sT", b))[0:N_EXP, :], ACT.Copy).then_inc(sT_ready, 1)
                    wait_bank(act, ("s3", b))
                    act.activation(s3T[:, :], bank(("s3", b))[0:3 * N_EXP, 0:256].bitcast(BF16),
                                   ACT.Copy).then_inc(sT_ready, 1)
                elif kind == "up":
                    b, e = step[1:]
                    wait_bank(act, step)
                    if b >= 1 and e == 0:
                        done(act, "down", TPB * b)
                    act.activation(hs[:, e, :], bank(step), ACT.Silu, bias=bup[:, e:e + 1]).then_inc(h_ready, 1)

        @block.vector
        def _(dve):
            chain = [0]

            def link(ins):
                chain[0] += 1
                ins.then_inc(dve_chain, 1)
                dve.wait_ge(dve_chain, chain[0])

            def stats(src, n):
                if n >= 2:
                    dve.wait_ge(xn_ready, n - 1)
                link(dve.bn_stats(bns[:, n % 2, :], src))
                dve.bn_aggr(mv[:, n % 2, :], bns[:, n % 2, :]).then_inc(var_ready, 1)

            def normalize(src, n):
                dve.wait_ge(rstd_ready, n + 1)
                dve.wait_ge(var_ready, n + 1)
                if n >= 4:
                    group, i = divmod(n - 4, TPB)
                    if i < TPB - 1:
                        dve.wait_ge(xn_used, (TPB - 1) * group + i + 1)
                    else:
                        wait_bank(dve, ("hT", group, 1) if group < BATCH else ("hid", group - BATCH, 1))
                dve.tensor_scalar(xn[:, n % 4, :], src, mv[:, n % 2, 0:1], rst[:, n % 2, 0:1],
                                  ALU.subtract, ALU.mult).then_inc(xn_ready, 1)

            out_of_range = [None]
            dve.wait_ge(ld["cst"], 48)
            dve.tensor_copy(sel[:, :, :], sel32.rearrange(
                "p (e c) -> p e c", e=N_EXP)).then_inc(consts_cast, 1)
            dve.tensor_copy(identb[:, :], ident).then_inc(consts_cast, 1)
            for step in STEPS:
                kind = step[0]
                if kind == "mod":
                    dve.wait_ge(csil_ready, 1)
                    dve.wait_ge(ld_x[0], 16)
                    stats(xin[:, 0, :], 0)
                    wait_bank(dve, "mod")
                    mod_ps = bank("mod")[:, 0:6 * KD * BATCH]
                    dve.tensor_copy(modT[:, :, :].rearrange("p m b -> p (m b)"), mod_ps).then_inc(mod_ready, 1)
                    dve.wait_ge(mod_ready, 1)
                    for a, which in enumerate((2, 5)):
                        g = modT[:, which * KD:(which + 1) * KD, :]
                        sgn = gsg[:, a]
                        link(dve.tensor_scalar(sgn, g, 0.0, 2.0, ALU.is_ge, ALU.mult))
                        link(dve.tensor_scalar(sgn, sgn, 1.0, None, ALU.subtract))
                        link(dve.tensor_tensor(g, g, sgn, ALU.mult))
                        link(dve.tensor_scalar(g, g, 0.25, None, ALU.max))
                        link(dve.tensor_tensor(g, g, sgn, ALU.mult))
                    for which in (1, 4):
                        m = modT[:, which * KD:(which + 1) * KD, :]
                        ins = dve.tensor_scalar(m, m, 1.0, None, ALU.add)
                        ins.then_inc(mod_ready, 1)
                elif kind == "ln1":
                    b = step[1]
                    for i in range(TPB):
                        n = tile_no(b, i)
                        if n + 1 < N_TILE:
                            dve.wait_ge(ld_x[(n + 1) // TPB], 16)
                            stats(xin[:, n + 1, :], n + 1)
                        normalize(xin[:, n, :], n)
                elif kind == "softplus":
                    for h in range(2):
                        s = slice(512 * h, 512 * h + 512)
                        dve.wait_ge(abs_ready, h + 1)
                        dve.tensor_scalar(sp_m[:, s], bank(("dt", h)), 0.0, None, ALU.max).then_inc(relu_ready, 1)
                    for h in range(2):
                        s = slice(512 * h, 512 * h + 512)
                        dve.wait_ge(expt_ready, h + 1)
                        dve.tensor_scalar(sp_w[:, s], sp_t[:, s], 1.0, None, ALU.add).then_inc(onep_ready, 1)
                    for h in range(2):
                        s = slice(512 * h, 512 * h + 512)
                        dve.wait_ge(ln_ready, h + 1)
                        link(dve.tensor_scalar(sp_w[:, s], sp_w[:, s], 1.0, TINY, ALU.subtract, ALU.add))
                        link(dve.reciprocal(sp_w[:, s], sp_w[:, s]))
                        link(dve.scalar_tensor_tensor(out=sp_l[:, s], in0=sp_l[:, s], scalar=TINY, in1=sp_t[:, s],
                                                      op0=ALU.add, op1=ALU.mult))
                        link(dve.tensor_tensor(sp_l[:, s], sp_l[:, s], sp_w[:, s], ALU.mult))
                        dve.wait_ge(relu_ready, h + 1)
                        dve.tensor_tensor(dt_f[:, s], sp_l[:, s], sp_m[:, s], ALU.add).then_inc(dt_ready, 1)
                elif kind == "factors":
                    h = step[1]
                    s = slice(512 * h, 512 * h + 512)
                    wait_bank(dve, ("E", h))
                    dve.wait_ge(dt_ready, 2)
                    dve.tensor_scalar(sp_l[:, s], bank(("E", h)), -RANGE, RANGE, ALU.max,
                                      ALU.min).then_inc(eclip_ready, 1)
                    dve.wait_ge(eclip_ready, h + 1)
                    dve.scalar_tensor_tensor(out=sp_w[:, s], in0=bank(("E", h)), scalar=1.0, in1=sp_l[:, s],
                                             op0=ALU.mult, op1=ALU.not_equal,
                                             accum_out=flg[:, h:h + 1]).then_inc(clip_counted, 1)
                elif kind == "gates":
                    b = step[1]
                    for a, (which, row) in enumerate(((2, b), (5, b - 1))):
                        if not 0 <= row < BATCH:
                            continue
                        for k in range(KD):
                            dve.tensor_scalar(scr[:, a, k * P:(k + 1) * P], ident,
                                              modT[:, which * KD + k, row:row + 1], None,
                                              ALU.mult).then_inc(diag_ready, 1)
                    wait_bank(dve, step)
                elif kind == "flag":
                    wait_bank(dve, "flag")
                    link(dve.tensor_reduce(flsum[:, :], bank("flag")[:, 0:2], AX.X, ALU.add))
                    dve.tensor_copy(flag[:, :], flsum[0:1, :]).then_inc(flag_ready, 1)
                    dve.wait_ge(flag_ready, 1)
                    out_of_range[0] = dve.value_load(flag[0:1, 0:1])
                    dve.wait_ge(ld["small"], 64)
                    for h in range(2):
                        s = slice(512 * h, 512 * h + 512)
                        fq_h = fq[:, 8 * h:8 * h + 8, :]
                        link(dve.reciprocal(fq_f[:, s], dt_f[:, s]))
                        dve.tensor_tensor(fq_h, fq_h, dh[:, None, :].to_broadcast([P, 8, N_HEAD]),
                                          ALU.mult).then_inc(q_ready, 1)
                elif kind == "proj":
                    b, m = step[1:]
                    if m < N_CONV:
                        c = N_CONV * b + m
                        dve.wait_ge(tap0, c + 1)
                        for s in range(1, KSIZE):
                            if s > 1:
                                dve.wait_ge(taps, 3 * c + s - 1)
                            dst = conv[:, b % 2, m, s:SEQ]
                            ins = dve.scalar_tensor_tensor(
                                out=dst, in0=bank(step)[:, 0:SEQ - s], scalar=cw[:, m, KSIZE - 1 - s:KSIZE - s],
                                in1=dst, op0=ALU.mult, op1=ALU.add)
                            ins.then_inc(taps, 1)
                elif kind == "tr":
                    b, i = step[1:]
                    n = tile_no(b, i)
                    if n >= 2:
                        done(dve, "y", n - 1)
                    for par in range(2):
                        job = ("cb", par, b, i)
                        wait_bank(dve, job)
                        dve.tensor_tensor(
                            gm[:, n % 2, par].rearrange("p (j s) -> p j s", s=CHUNK),
                            bank(job)[:, 0:4 * CHUNK].rearrange("p (j s) -> p j s", s=CHUNK),
                            cst[:, None, C_TRI:C_TRI + CHUNK].to_broadcast([P, 4, CHUNK]),
                            ALU.mult).then_inc(gm_ready, 1)
                elif kind == "state":
                    b, i = step[1:]
                    n = tile_no(b, i)
                    for c in range(2):
                        job = ("st", c, b, i)
                        if job not in bank_of:
                            continue
                        k = chunks_before(b, i) + c
                        wait_bank(dve, job)
                        d = dec[:, n, c, :, None].to_broadcast([P, 32, HEAD])
                        new = st[:, k % 4, :].rearrange("p (h d) -> p h d", d=HEAD)
                        if n >= 1:
                            done(dve, "y", n)
                        pst = bank(job)[:, 0:4 * CHUNK]
                        dve.wait_ge(dec_ready, 8)
                        if i == 0 and c == 0:
                            dve.tensor_tensor(new, pst.rearrange("p (h d) -> p h d", d=HEAD), d,
                                              ALU.mult).then_inc(st_ready, 1)
                        else:
                            dve.wait_ge(st_ready, k)
                            link(dve.tensor_tensor(scr[:, 0, :], pst, st[:, (k - 1) % 4, :], ALU.add))
                            dve.tensor_tensor(new, scr[:, 0, :].rearrange("p (h d) -> p h d", d=HEAD), d,
                                              ALU.mult).then_inc(st_ready, 1)
                elif kind == "y":
                    b, i = step[1:]
                    n = tile_no(b, i)
                    if n >= 2:
                        done(dve, "z", n - 1)
                    for par in range(2):
                        job = ("y", par, b, i)
                        wait_bank(dve, job)
                        dst = ytok[:, n % 2, :].rearrange("p (j a h d) -> p a j h d", a=2, h=8, d=HEAD)[:, par]
                        u = fu[:, n, :].rearrange("p (j a h) -> p a j h", a=2, h=8)[:, par]
                        dve.tensor_tensor(dst, bank(job)[:, 0:4 * CHUNK].rearrange("p (j h d) -> p j h d", h=8, d=HEAD),
                                          u[:, :, :, None].to_broadcast([P, CT_, 8, HEAD]),
                                          ALU.mult).then_inc(ytok_ready, 1)
                    with dve.If(out_of_range[0] > 0):
                        general_dve(dve, b, i)
                elif kind == "z":
                    b, i = step[1:]
                    n = tile_no(b, i)
                    wait_bank(dve, step)
                    if n >= 2:
                        done(dve, "out", n - 1)
                    dve.wait_ge(silu_done, N_PROJ * (b + 1))
                    dve.tensor_tensor(yT[:, n % 2], bank(step)[:, :].rearrange("p (m t) -> p m t", t=P),
                                      sz[:, :, i * P:(i + 1) * P],
                                      ALU.mult).then_inc(yT_ready, 1)
                elif kind == "out":
                    b, i = step[1:]
                    n = tile_no(b, i)
                    wait_bank(dve, step)
                    dve.wait_ge(ld_res[b % 2], 16 * (b // 2 + 1))
                    r = x1[:, b % 2, i, :]
                    dve.tensor_tensor(r, bank(step)[:, 0:DM], r, ALU.add).then_inc(x1_ready, 1)
                    dve.wait_ge(x1_ready, n + 1)
                    stats(r, N_TILE + n)
                elif kind == "norm":
                    b, i = step[1:]
                    normalize(x1[:, b % 2, i, :], N_TILE + tile_no(b, i))
                elif kind == "gate2":
                    b = step[1]
                    wait_bank(dve, step)
                    dve.tensor_copy(lg[:, :, :].rearrange("p i e -> p (i e)"),
                                    bank(step)[:, 0:TPB * N_EXP]).then_inc(lg_ready, 1)
                    dve.wait_ge(lg_ready, b + 1)
                    for i in range(TPB):
                        ins = dve.max(top[:, i, :], lg[:, i, :])
                        chain[0] += 1
                        ins.then_inc(dve_chain, 1)
                    mine = lg[:, :, :, None].to_broadcast([P, TPB, N_EXP, N_EXP])
                    other = lg[:, :, None, :].to_broadcast([P, TPB, N_EXP, N_EXP])
                    for dst, op in ((cmp_, ALU.is_gt), (eq, ALU.is_equal)):
                        ins = dve.tensor_tensor(dst[:, :, :, :], other, mine, op)
                        chain[0] += 1
                        ins.then_inc(dve_chain, 1)
                    dve.wait_ge(dve_chain, chain[0])
                    tri8 = cst[:, None, C_RANK:C_RANK + 64].to_broadcast([P, TPB, 64])
                    eqf = eq[:, :, :, :].rearrange("p i a b -> p i (a b)")
                    cmf = cmp_[:, :, :, :].rearrange("p i a b -> p (i a b)")
                    link(dve.tensor_tensor(eqf, eqf, tri8, ALU.mult))
                    link(dve.tensor_tensor(cmf, cmf, eq[:, :, :, :].rearrange("p i a b -> p (i a b)"), ALU.add))
                    link(dve.tensor_reduce(rank[:, :, :].rearrange("p i a -> p (i a)"),
                                           cmp_[:, :, :, :].rearrange("p i a b -> p (i a) b"), AX.X, ALU.add))
                    link(dve.tensor_scalar(rank[:, :, :], rank[:, :, :], 1.5, 0.5, ALU.is_lt, ALU.mult))
                    link(dve.tensor_tensor(msum[:, :], top[:, :, 0], top[:, :, 1], ALU.add))
                    dve.scalar_tensor_tensor(out=dl[:, :, :], in0=lg[:, :, :], scalar=2.0,
                                             in1=msum[:, :, None].to_broadcast([P, TPB, N_EXP]),
                                             op0=ALU.mult, op1=ALU.subtract).then_inc(dl_ready, 1)
                elif kind == "score":
                    b = step[1]
                    dve.wait_ge(tl_ready, b + 1)
                    link(dve.scalar_tensor_tensor(out=sc[:, :, :], in0=tl[:, :, :], scalar=1.0, in1=rank[:, :, :],
                                                  op0=ALU.add, op1=ALU.mult))
                    link(dve.tensor_copy(s3[:, :, 0, :], sc[:, :, :]))
                    link(dve.tensor_tensor(dl[:, :, :], sc[:, :, :], s3[:, :, 0, :], ALU.subtract))
                    link(dve.tensor_copy(s3[:, :, 1, :], dl[:, :, :]))
                    dve.tensor_tensor(s3[:, :, 2, :], dl[:, :, :], s3[:, :, 1, :], ALU.subtract).then_inc(sc_ready, 1)
                elif kind == "up":
                    b, e = step[1:]
                    k = b * N_EXP + e
                    job = ("bc", b, e)
                    wait_bank(dve, job)
                    dve.wait_ge(h_ready, k + 1)
                    dve.tensor_tensor(hs[:, e, :], hs[:, e, :], bank(job), ALU.mult).then_inc(hs_ready, 1)
                elif kind == "down":
                    b, i = step[1:]
                    n = tile_no(b, i)
                    wait_bank(dve, step)
                    r = x1[:, b % 2, i, :]
                    dve.wait_ge(xn_ready, N_TILE + n + 1)
                    dve.tensor_tensor(r, bank(step)[:, 0:DM], r, ALU.add).then_inc(x2_ready, 1)

        @block.tensor
        def _(pe):
            def tile_cols(i):
                return slice(i * P, (i + 1) * P)

            def transpose_norm(b, name):
                first = 0 if name == "hT" else N_TILE
                for i in range(TPB):
                    n = first + tile_no(b, i)
                    pe.wait_ge(xn_ready, n + 1)
                    for k in range(KD):
                        job = (name, b, k)
                        if i == 0:
                            wait_bank_free(pe, job)
                        ins = pe.transpose(bank(job)[:, tile_cols(i)], xn[:, n % 4, k * P:(k + 1) * P], ident)
                        if i == TPB - 1:
                            ins.then_inc(full[bank_of[job]], 1)
                        elif k == KD - 1:
                            ins.then_inc(xn_used, 1)

            out_of_range = [None]
            pe.wait_ge(ld["cst"], 48)
            for step in STEPS:
                kind = step[0]
                if kind == "mod":
                    pe.wait_ge(ld["wmod"], 16)
                    pe.wait_ge(csil_ready, 1)
                    for m in range(6 * KD):
                        for k in range(KD):
                            ins = pe.matmul(bank("mod")[:, m * BATCH:(m + 1) * BATCH], wmod[:, k, m * P:(m + 1) * P],
                                            csil[:, k, :], start=(k == 0), stop=(k == KD - 1))
                    ins.then_inc(full[bank_of["mod"]], 1)
                elif kind == "ln1":
                    transpose_norm(step[1], "hT")
                elif kind == "dt":
                    h = step[1]
                    job = ("dt", h)
                    pe.wait_ge(ld["win"], 16)
                    wait_bank_free(pe, job)
                    for i in range(8):
                        n = 8 * h + i
                        pe.wait_ge(hT_ready, KD * (n // TPB + 1))
                        for k in range(KD):
                            ins = pe.matmul(bank(job)[:, i * N_HEAD:(i + 1) * N_HEAD], hT[:, k, tile_cols(n)],
                                            win[:, k, 4 * DI:N_IN], start=(k == 0), stop=(k == KD - 1))
                    ins.then_inc(full[bank_of[job]], 1)
                elif kind == "factors":
                    h = step[1]
                    job = ("E", h)
                    pe.wait_ge(dt_ready, h + 1)
                    wait_bank_free(pe, job)
                    pe.matmul(bank(job), early[:, E_MID:E_MID + P], dt_f[:, 512 * h:512 * h + 512],
                              start=True, stop=True).then_inc(full[bank_of[job]], 1)
                elif kind == "decays":
                    pe.wait_ge(dt_ready, 2)
                    for n in range(4):
                        job = ("D", n)
                        wait_bank_free(pe, job)
                        lo = 512 * (n % 2)
                        cnt = 512 if n < 3 else 448
                        if n < 2:
                            ins = pe.matmul(bank(job), early[:, E_AB:E_AB + P], dt_f[:, lo:lo + cnt], start=True, stop=True)
                        else:
                            pe.matmul(bank(job)[:, 0:cnt], early[:, E_BH:E_BH + P], dt_f[:, lo:lo + cnt],
                                      start=True, stop=False)
                            ins = pe.matmul(bank(job)[:, 0:cnt], early[:, E_AL:E_AL + P],
                                            dt_f[:, lo + N_HEAD:lo + N_HEAD + cnt], start=False, stop=True)
                        ins.then_inc(full[bank_of[job]], 1)
                elif kind == "flag":
                    pe.wait_ge(clip_counted, 2)
                    wait_bank_free(pe, "flag")
                    pe.matmul(bank("flag")[:, 0:2], cst[:, C_ONE:C_ONE + P], flg[:, :],
                              start=True, stop=True).then_inc(full[bank_of["flag"]], 1)
                    pe.wait_ge(flag_ready, 1)
                    out_of_range[0] = pe.value_load(flag[0:1, 0:1])
                elif kind == "proj":
                    b, m = step[1:]
                    wait_bank_free(pe, step)
                    for k in range(KD):
                        ins = pe.matmul(bank(step), win[:, k, m * P:(m + 1) * P], hT[:, k, b * SEQ:(b + 1) * SEQ],
                                        start=(k == 0), stop=(k == KD - 1))
                    ins.then_inc(full[bank_of[step]], 1)
                elif kind == "gates":
                    b = step[1]
                    wait_bank_free(pe, step)
                    made = KD * (2 * b + 1) if b < BATCH else 2 * KD * b
                    pe.wait_ge(diag_ready, made)
                    for a, row in enumerate((b, b - 1)):
                        if not 0 <= row < BATCH:
                            continue
                        for k in range(KD):
                            ins = pe.matmul(bank(step)[:, a * DM + k * P:a * DM + (k + 1) * P],
                                            cst[:, C_ONE:C_ONE + P], scr[:, a, k * P:(k + 1) * P],
                                            start=True, stop=True)
                    ins.then_inc(full[bank_of[step]], 1)
                elif kind == "tr":
                    b, i = step[1:]
                    pe.wait_ge(silu_done, N_PROJ * b + N_CONV)
                    for job, base in ((("xt", b, i), 0), (("bt", b, i), CT_)):
                        wait_bank_free(pe, job)
                        for j in range(CT_):
                            ins = pe.transpose(bank(job)[:, tile_cols(j)], conv[:, b % 2, base + j, tile_cols(i)], ident)
                        ins.then_inc(full[bank_of[job]], 1)
                        if base == 0:
                            for par in range(2):
                                rows = slice(64 * par, 64 * par + 64)
                                job = ("cb", par, b, i)
                                wait_bank_free(pe, job)
                                for j in range(CT_):
                                    for c in range(2):
                                        t = slice(i * P + c * CHUNK, i * P + (c + 1) * CHUNK)
                                        ins = pe.matmul(
                                            ps[64 * c:64 * c + 64, bank_of[job], j * CHUNK:(j + 1) * CHUNK],
                                            conv[rows, b % 2, CT_ + j, t], conv[rows, b % 2, 2 * CT_ + j, t],
                                            start=True, stop=True)
                                ins.then_inc(full[bank_of[job]], 1)
                elif kind == "state":
                    b, i = step[1:]
                    n = tile_no(b, i)
                    pe.wait_ge(btok_ready, n + 1)
                    pe.wait_ge(xv_ready, n + 1)
                    for c in range(2):
                        job = ("st", c, b, i)
                        if job not in bank_of:
                            continue
                        rows = slice(64 * c, 64 * c + 64)
                        wait_bank_free(pe, job)
                        for g in range(N_GRP):
                            j, par = g // 2, g % 2
                            ins = pe.matmul(ps[64 * par:64 * par + 64, bank_of[job], j * CHUNK:(j + 1) * CHUNK],
                                            btok[rows, n % 2, g * 64:(g + 1) * 64],
                                            xv[rows, n % 2, g * 64:(g + 1) * 64], start=True, stop=True)
                        ins.then_inc(full[bank_of[job]], 1)
                elif kind == "y":
                    b, i = step[1:]
                    n = tile_no(b, i)
                    pe.wait_ge(gm_ready, 2 * n + 2)
                    pe.wait_ge(st_ready, chunks_before(b, i) + 1)
                    for par in range(2):
                        wait_bank_free(pe, ("y", par, b, i))
                    for par in range(2):
                        rows = slice(64 * par, 64 * par + 64)
                        for c in range(2):
                            if i == 0 and c == 0:
                                continue
                            k = chunks_before(b, i) + c - 1
                            t = slice(i * P + c * CHUNK, i * P + (c + 1) * CHUNK)
                            for j in range(CT_):
                                ins = pe.matmul(
                                    ps[64 * c:64 * c + 64, bank_of[("y", par, b, i)], j * CHUNK:(j + 1) * CHUNK],
                                    conv[rows, b % 2, 2 * CT_ + j, t], st[rows, k % 4, j * CHUNK:(j + 1) * CHUNK],
                                    start=(j == 0), stop=False, skip_group_check=True)
                    ins.then_inc(yo_done, 1)
                    pe.wait_ge(yo_done, n + 1)
                    for par in range(2):
                        job = ("y", par, b, i)
                        for c in range(2):
                            rows = slice(64 * c, 64 * c + 64)
                            for j in range(CT_):
                                g = 2 * j + par
                                last = pe.matmul(
                                    ps[rows, bank_of[job], j * CHUNK:(j + 1) * CHUNK],
                                    gm[rows, n % 2, par, j * CHUNK:(j + 1) * CHUNK],
                                    xv[rows, n % 2, g * 64:(g + 1) * 64],
                                    start=(i == 0 and c == 0 and j == 0), stop=True, skip_group_check=True)
                        if par == 0:
                            last.then_inc(full[bank_of[job]], 1)
                    job = ("y", 1, b, i)
                    last.then_inc(full[bank_of[job]], 1)
                    with pe.If(out_of_range[0] > 0):
                        general_pe(pe, b, i)
                elif kind == "z":
                    b, i = step[1:]
                    n = tile_no(b, i)
                    wait_bank_free(pe, step)
                    pe.wait_ge(ytok_ready, 2 * n + 2)
                    pe.wait_ge(xq_ready, n + 1)
                    for m in range(CT_):
                        out = bank(step)[:, tile_cols(m)]
                        pe.matmul(out, ytok[:, n % 2, tile_cols(m)], ident, is_transpose=True, start=True, stop=False)
                        ins = pe.matmul(out, xtok[:, n % 2, tile_cols(m)], ident, is_transpose=True,
                                        start=False, stop=True)
                    ins.then_inc(full[bank_of[step]], 1)
                elif kind == "out":
                    b, i = step[1:]
                    n = tile_no(b, i)
                    wait_bank_free(pe, step)
                    pe.wait_ge(yT_ready, n + 1)
                    pe.wait_ge(wog_ready, b + 1)
                    for m in range(CT_):
                        ins = pe.matmul(bank(step)[:, 0:DM], yT[:, n % 2, m, :], wog[:, m, :],
                                        start=(m == 0), stop=(m == CT_ - 1))
                    ins.then_inc(full[bank_of[step]], 1)
                elif kind == "hid":
                    transpose_norm(step[1], "hid")
                elif kind == "gate1":
                    b = step[1]
                    wait_bank_free(pe, step)
                    pe.wait_ge(hid_ready, KD * (b + 1))
                    pe.wait_ge(ld["ffn"], 48)
                    for k in range(KD):
                        ins = pe.matmul(bank(step)[0:N_EXP, :], wg1[:, k, :], hT[:, k, b * SEQ:(b + 1) * SEQ],
                                        start=(k == 0), stop=(k == KD - 1))
                    ins.then_inc(full[bank_of[step]], 1)
                elif kind == "gate2":
                    b = step[1]
                    wait_bank_free(pe, step)
                    pe.wait_ge(th_ready, b + 1)
                    for i in range(TPB):
                        ins = pe.matmul(bank(step)[:, i * N_EXP:(i + 1) * N_EXP], th[:, tile_cols(i)], wg2[:, :],
                                        start=True, stop=True)
                    ins.then_inc(full[bank_of[step]], 1)
                elif kind == "spread":
                    b = step[1]
                    pe.wait_ge(sc_ready, b + 1)
                    job = ("sT", b)
                    wait_bank_free(pe, job)
                    for i in range(TPB):
                        ins = pe.transpose(bank(job)[0:N_EXP, tile_cols(i)], sc[:, i, :], ident)
                    ins.then_inc(full[bank_of[job]], 1)
                    job = ("s3", b)
                    wait_bank_free(pe, job)
                    pe.wait_ge(consts_cast, 2)
                    dst = bank(job)[0:3 * N_EXP, 0:256].bitcast(BF16)
                    for i in range(TPB):
                        ins = pe.transpose(dst[:, tile_cols(i)], s3[:, i].rearrange("p a e -> p (a e)"), identb[:, :])
                    ins.then_inc(full[bank_of[job]], 1)
                elif kind == "up":
                    b, e = step[1:]
                    wait_bank_free(pe, step)
                    pe.wait_ge(ld["wup"], 16)
                    for k in range(KD):
                        ins = pe.matmul(bank(step), wup[:, k, e * P:(e + 1) * P], hT[:, k, b * SEQ:(b + 1) * SEQ],
                                        start=(k == 0), stop=(k == KD - 1))
                    ins.then_inc(full[bank_of[step]], 1)
                    job = ("bc", b, e)
                    wait_bank_free(pe, job)
                    pe.wait_ge(sT_ready, 2 * b + 2)
                    pe.matmul(bank(job), sel[:, e, :], s3T[:, :], start=True, stop=True).then_inc(
                        full[bank_of[job]], 1)
                elif kind == "down":
                    b, i = step[1:]
                    wait_bank_free(pe, step)
                    pe.wait_ge(wdg_ready, 2 * (b + 1))
                    out = bank(step)[:, 0:DM]
                    pe.matmul(out, sT[:, tile_cols(i)], bdg[:, :], start=True, stop=False)
                    for e in range(N_EXP):
                        pe.wait_ge(hs_ready, b * N_EXP + e + 1)
                        ins = pe.matmul(out, hs[:, e, tile_cols(i)], wdg[:, e, :], start=False, stop=(e == N_EXP - 1))
                    ins.then_inc(full[bank_of[step]], 1)


def _shape_constants():
    import numpy as np
    c = np.zeros((P, C_ALL), np.float32)
    early = np.zeros((P, E_ALL), np.float32)
    k = np.arange(P)[:, None]
    t = np.arange(P)[None, :]
    c[:, C_ID:C_ID + P] = np.eye(P)
    same = k // CHUNK == t // CHUNK
    kk, tt, mid = k % CHUNK, t % CHUNK, CHUNK // 2
    early[:, E_MID:E_MID + P] = same * (((tt >= mid) & (kk >= mid) & (kk <= tt)) * 1.0
                                    - ((tt < mid) & (kk < mid) & (kk > tt)) * 1.0)
    rows = np.arange(P)[:, None] * np.ones((1, P))
    early[:, E_AB:E_AB + P] = (rows >= mid) & (rows < CHUNK + mid)
    early[:, E_BH:E_BH + P] = rows >= CHUNK + mid
    early[:, E_AL:E_AL + P] = rows < mid
    c[:, C_TRI:C_TRI + CHUNK] = (k % CHUNK) <= np.arange(CHUNK)[None, :]
    s = np.zeros((P, N_EXP, P), np.float32)
    for e in range(N_EXP):
        for part in range(3):
            s[part * N_EXP + e, e, :] = 1.0
    sel = s[0:3 * N_EXP].reshape(3 * N_EXP, N_EXP * P)
    e = np.arange(N_EXP)
    c[:, C_RANK:C_RANK + 64] = (e[None, :] < e[:, None]).astype(np.float32).reshape(1, 64)
    c[:, C_ONE:C_ONE + P] = 1.0
    return c, early, sel


def _general_tables():
    import numpy as np
    k = np.arange(P)[:, None]
    t = np.arange(P)[None, :]
    g = np.zeros((LEVELS + 1, P, 3, P), np.float32)
    for lv in range(LEVELS - 1):
        size = P >> (lv + 1)
        ref = t // (2 * size) * (2 * size) + size - 1
        later = t // size % 2 == 1
        w = (later & (k > ref) & (k <= t)) | (~later & (k > t) & (k <= ref))
        g[lv, :, 0] = g[lv, :, 1] = w
        g[lv, :, 2] = (k // (2 * size) == t // (2 * size)) & (k // size % 2 == 0) & later
    g[LEVELS - 1, :, 2] = k == t
    g[LEVELS, :, 0] = k > t
    g[LEVELS, :, 1] = k <= t
    g[LEVELS, :, 2] = 1.0
    return g.reshape(LEVELS + 1, P, 3 * P)


def kernel(**inputs):
    import numpy as np
    import concourse.bacc as bacc
    from concourse.bass_utils import run_bass_kernel_spmd

    a = {k: np.asarray(v) for k, v in inputs.items()}
    cont = np.ascontiguousarray

    def by_tile(v):
        return cont(np.moveaxis(v.reshape((-1, P) + v.shape[1:]), 0, 1))

    arrays = {
        "x": cont(a["L0_attn_input_"]),
        "c_T": cont(a["L0_c"].T),
        "w_mod": cont(a["L0_wmod"]),
        "w_in_T": cont(a["L0_attn_in_proj_w"].T),
        "w_conv": by_tile(a["L0_attn_conv1d_weight"][:, 0, :]),
        "b_conv": by_tile(a["L0_attn_conv1d_bias"]),
        "b_z": by_tile(a["L0_attn_z_bias"]),
        "d_head": cont(np.broadcast_to(a["L0_attn_D"], (P, N_HEAD))),
        "w_out_T": cont(a["L0_attn_out_proj_w"].T),
        "w_g1_T": cont(a["L0_ffn_Wg1"].T),
        "w_g2_T": cont(a["L0_ffn_Wg2"].T),
        "w_up_T": cont(a["L0_ffn_Wup"].reshape(N_EXP * D_EXP, DM).T),
        "b_up": cont(a["L0_ffn_bup"].T),
        "w_down_T": cont(a["L0_ffn_Wdown"].transpose(0, 2, 1)),
        "b_down": cont(a["L0_ffn_bdown"]),
        "shape_consts": _shape_constants()[0],
        "early_consts": _shape_constants()[1],
        "expert_rows": _shape_constants()[2],
        "general_tables": _general_tables(),
    }
    nc = bacc.Bacc("TRN2", target_bir_lowering=False, num_devices=1)
    args = [nc.dram_tensor(n, v.shape, mybir.dt.from_np(v.dtype), kind="ExternalInput").ap()
            for n, v in arrays.items()]
    args.append(nc.dram_tensor("out", (BATCH, SEQ, DM), F32, kind="ExternalOutput").ap())
    adaln_block(nc, *args)
    r = run_bass_kernel_spmd(nc, [arrays], core_ids=[0])
    return r.results[0]["out"]
```

```python
from contextlib import ExitStack

import concourse.bass as bass
from concourse import mybir

P = 128
BATCH, SEQ, DM = 4, 512, 256
DI, N_HEAD, HEAD, N_GRP, D_STATE = 512, 64, 8, 8, 64
KSIZE = 4
CHUNK = 64
N_EXP, D_EXP = 8, 128
TOK = BATCH * SEQ
N_TILE = TOK // P
TPB = SEQ // P
KD = DM // P
CT_ = DI // P
N_PROJ = 4 * CT_
N_CONV = 3 * CT_
N_IN = 4 * DI + N_HEAD
EPS = 1e-5
RANGE = 60.0
G_BANK = 2
WARM_UP = 4
WARM_BANK = 7
ROW_0_ORDER = (0, 1, 2, 3, 12, 13, 4, 5, 6, 7, 8, 9, 10, 11, 14, 15)
LEVELS = 8

F32 = mybir.dt.float32
BF16 = mybir.dt.bfloat16
I32 = mybir.dt.int32
ALU = mybir.AluOpType
ACT = mybir.ActivationFunctionType
AX = mybir.AxisListType

C_ID, C_ONE, C_TRI, C_RANK = 0, P, 2 * P, 2 * P + CHUNK
C_ALL = C_RANK + N_EXP * N_EXP
E_MID, E_AB, E_BH, E_AL = 0, P, 2 * P, 3 * P
E_ALL = 4 * P
S_CB = N_CONV * KSIZE
S_ZB = S_CB + N_CONV
S_D = S_ZB + CT_
S_ALL = S_D + N_HEAD
MOD_TILES = ((0, 2 * KD), (2 * KD, 6 * KD))


def program_order():
    def proj(b, *tiles):
        return [("proj", b, m) for m in tiles]

    z_tiles = range(N_CONV, N_PROJ)
    steps = [("ln1", 0), ("mod", 0), ("ln1", 1), *proj(0, 0), ("ln1", 2), *proj(0, 1), ("ln1", 3),
             ("dt", 0), *proj(0, 2), ("dt", 1), ("abs", 0), ("abs", 1), *proj(0, 3), ("exp", 0), ("exp", 1),
             *proj(0, z_tiles[0]), ("mod", 1), *proj(0, z_tiles[1]), ("log", 0), ("log", 1), *proj(0, 4),
             ("factors", 0), ("factors", 1), *proj(0, 5), ("decays",), ("flag",), *proj(0, 6), *proj(0, 7),
             ("diag", 0), *proj(0, 8), ("gates", 0), *proj(0, 9), *proj(0, 10), *proj(0, 11),
             *proj(0, z_tiles[2]), ("d_dt", 0), *proj(0, z_tiles[3])]
    for slot in range(BATCH + 1):
        nxt = [("proj", slot + 1, m) for m in range(N_CONV)] if slot + 1 < BATCH else []
        z_own = [("proj", slot, m) for m in z_tiles] if 0 < slot < BATCH else []
        down = [("down", slot - 2, i) for i in range(TPB)] if slot >= 2 else []
        last_bc = [("bc", slot - 2, N_EXP - 1)] if slot >= 2 else []
        b = slot - 1
        if slot == BATCH:
            steps += [*last_bc, ("z", b, TPB - 1), down[0], ("out", b, TPB - 1), down[1], ("norm", b, TPB - 1), down[2],
                      ("hid", b), down[3], ("up", b, 0), ("gate1", b), ("up", b, 1), ("gate2", b), ("up", b, 2),
                      ("fold_down", b), ("up", b, 3), ("up", b, 4), ("score", b), ("up", b, 5), ("spread", b),
                      ("up", b, 6), ("bc", b, 0), ("up", b, 7)]
            steps += [("bc", b, e) for e in range(1, N_EXP)] + [("down", b, i) for i in range(TPB)]
            break
        for i in range(TPB):
            prev = (slot, i - 1) if i else (b, TPB - 1)
            gap = 0
            for kind in ("tr", "", "bt", "z", "", "state", "", "out", "", "norm", "y", ""):
                if not kind:
                    steps += filling(slot, i, gap, nxt, z_own, last_bc, down)
                    gap += 1
                elif kind in ("z", "out", "norm"):
                    if prev[0] >= 0:
                        steps.append((kind,) + prev)
                else:
                    steps.append((kind, slot, i))
                if (slot, i, kind) == (0, 2, "y"):
                    steps.append(("d_dt", 1))
                if i == 0 and kind == "y":
                    steps.append(("fold_out", slot))
                if i == TPB - 1 and kind == "state":
                    steps.append(("diag", slot + 1))
                if i == TPB - 1 and kind == "norm":
                    steps.append(("gates", slot + 1))
    return steps


GAPS = (("hid p", "p 0", "p gate1", "1 p", "gate2 p"),
        ("2 fold_down p", "3 score p", "p spread", "4 p", "b0 5"),
        ("b1 p", "b2 6", "b3 7", "b4 p b5", "b6"))


def filling(slot, i, gap, nxt, z_own, last_bc, down):
    def take(steps, count=1):
        return [steps.pop(0) for _ in range(min(int(count), len(steps)))]

    if slot == 0:
        return take(nxt, gap in ((0, 1, 3) if i < TPB - 1 else (0, 1, 2)))
    if i == 0:
        return take(last_bc) + take(nxt) if gap == 0 else take(z_own) + take(down)
    out = []
    for word in GAPS[i - 1][gap].split():
        if word == "p":
            out += take(nxt)
        elif word.isdigit():
            out.append(("up", slot - 1, int(word)))
        elif word[0] == "b":
            out.append(("bc", slot - 1, int(word[1])))
        else:
            out.append((word, slot - 1))
    return out


def bank_jobs(step, tail):
    kind = step[0]
    ffn = [7, 2, 0, 1, 3, 4, 5, 6] if tail else [7, 2]
    if kind == "mod":
        return {step: (7, 2)[step[1]]}
    if kind == "ln1":
        return {("hT", step[1], k): 2 + 2 * (step[1] % 2) + k for k in range(KD)}
    if kind == "dt":
        return {("dt", step[1]): 6 + step[1]}
    if kind == "factors":
        return {("E", step[1]): 6}
    if kind == "decays":
        return {("D", n): (2, 3, 4, 5)[n] for n in range(4)}
    if kind == "flag":
        return {"flag": 7}
    if kind == "proj":
        m = step[2]
        if step[1] == 0:
            n = ROW_0_ORDER.index(m)
            return {step: n % 2 if n < 8 else (0, 1, 6)[n % 3]}
        if step[1] == 1 and m < N_CONV:
            return {step: (0, 1, 7)[m % 3] if m < N_CONV - 1 else 0}
        return {step: m % 2 if m < N_CONV else (m + 1) % 2}
    if kind == "gates":
        return {step: 7}
    if kind == "tr":
        return {("xt",) + step[1:]: 2, ("cb", 0) + step[1:]: 3, ("cb", 1) + step[1:]: 4}
    if kind == "bt":
        return {step: 2}
    if kind == "state":
        jobs = {("st", 0) + step[1:]: 3, ("st", 1) + step[1:]: 4}
        if step[2] == TPB - 1:
            del jobs[("st", 1) + step[1:]]
        return jobs
    if kind == "y":
        return {("y", 0) + step[1:]: 5, ("y", 1) + step[1:]: 6}
    if kind == "z":
        return {step: 5}
    if kind == "out":
        return {step: 6}
    if kind == "hid":
        return {("hid", step[1], 0): 7, ("hid", step[1], 1): 2}
    if kind in ("gate1", "gate2"):
        return {step: 2}
    if kind == "spread":
        return {("sT", step[1]): 7, ("s3", step[1]): 2}
    if kind == "up":
        return {step: ffn[2 * step[2] % len(ffn)]}
    if kind == "bc":
        return {step: ffn[(2 * step[2] + 1) % len(ffn)] if tail else (2 if step[2] < 6 else 7)}
    if kind == "down":
        return {step: ffn[(3 + step[2]) % len(ffn)] if tail else 7}
    return {}


def adaln_block(nc, x_d, cT_d, wmod_d, win_d, small_d, wo_d, wg1_d, wg2_d,
                wup_d, bup_d, wdn_d, bdn_d, const_d, early_d, sel_d, gen_d, out_d):
    STEPS = program_order()
    tail_from = max(n for n, s in enumerate(STEPS) if s[0] in ("out", "norm"))
    bank_of, use_no, used = {}, {}, [0] * 8
    for n, step in enumerate(STEPS):
        for job, bank in bank_jobs(step, n > tail_from).items():
            bank_of[job], use_no[job] = bank, used[bank]
            used[bank] += 1
    g_after = {}
    for n, step in enumerate(STEPS):
        for job, bank in bank_jobs(step, n > tail_from).items():
            if bank == G_BANK:
                last_job = job
        if step[0] == "y":
            g_after[step[1:]] = last_job

    with ExitStack() as ctx:
        def sb(name, shape, dt=F32):
            return ctx.enter_context(nc.sbuf_tensor(name, shape, dt))

        def sem(name):
            return ctx.enter_context(nc.semaphore(name))

        ps = ctx.enter_context(nc.psum_tensor("ps", [P, 8, 512], F32))

        cst = sb("cst", [P, C_ALL])
        win = sb("win", [P, KD, N_IN])
        small = sb("small", [P, S_ALL])
        cw = small[:, 0:S_CB].rearrange("p (m t) -> p m t", t=KSIZE)
        cb = small[:, S_CB:S_ZB]
        zb = small[:, S_ZB:S_D]
        dh = small[:, S_D:S_ALL]
        wog = sb("wog", [P, CT_, DM])
        wg1 = sb("wg1", [P, KD, N_EXP])
        wg2 = sb("wg2", [N_EXP, N_EXP])
        wup = sb("wup", [P, KD, N_EXP * D_EXP])
        bup = sb("bup", [P, N_EXP])
        wdg = sb("wdg", [P, N_EXP, DM])
        bdg = sb("bdg", [N_EXP, DM])
        sel = sb("sel", [3 * N_EXP, N_EXP, P], BF16)
        identb = sb("identb", [P, P], BF16)
        half = sb("half", [P, 1])
        csb = sb("csb", [P, KD, BATCH])
        csil = sb("csil", [P, KD, BATCH])
        modT = sb("modT", [P, 6 * KD, BATCH])
        gates = sb("gates", [P, 2, DM])
        gsg = sb("gsg", [P, 2, KD, BATCH])
        hT = sb("hT", [P, KD, TOK])
        x1 = sb("x1", [P, 2, TPB, DM])
        conv = sb("conv", [P, 2, N_CONV, SEQ])
        sz = sb("sz", [P, CT_, SEQ])
        dt = sb("dt", [P, N_TILE, N_HEAD])
        fu = sb("fu", [P, N_TILE, N_HEAD])
        fv = sb("fv", [P, N_TILE, N_HEAD])
        fq = sb("fq", [P, N_TILE, N_HEAD])
        dec = sb("dec", [P, N_TILE, 2, N_HEAD // 2])
        flg = sb("flg", [P, 2])
        flsum = sb("flsum", [P, 1])
        flag = sb("flag", [1, 1], I32)
        xtok = sb("xtok", [P, 2, DI])
        xv = sb("xv", [P, 2, DI])
        btok = sb("btok", [P, 2, DI])
        gm = sb("gm", [P, 2, 2, 4 * CHUNK])
        ytok = sb("ytok", [P, 2, DI])
        yT = sb("yT", [P, 2, CT_, P])
        st = sb("st", [P, 4, 4 * CHUNK])
        scr = sb("scr", [P, 2, KD * P])
        xn = sb("xn", [P, 4, DM])
        bns1 = sb("bns1", [P, 2, TPB, 6])
        mv1 = sb("mv1", [P, N_TILE, 2])
        rst1 = sb("rst1", [P, N_TILE, 1])
        bns = sb("bns", [P, 2, 6])
        mv = sb("mv", [P, 2, 2])
        rst = sb("rst", [P, 2, 1])
        hs = sb("hs", [P, N_EXP, SEQ])
        lg = sb("lg", [P, TPB, N_EXP])
        top = sb("top", [P, TPB, N_EXP])
        cmp_ = sb("cmp", [P, TPB, N_EXP, N_EXP])
        eq = sb("eq", [P, TPB, N_EXP, N_EXP])
        rank = sb("rank", [P, TPB, N_EXP])
        msum = sb("msum", [P, TPB])
        dl = sb("dl", [P, TPB, N_EXP])
        tl = sb("tl", [P, TPB, N_EXP])
        sc = sb("sc", [P, TPB, N_EXP])
        s3 = sb("s3", [P, TPB, 3, N_EXP], BF16)
        sT = sb("sT", [N_EXP, SEQ])
        th = sT
        s3T = sb("s3T", [3 * N_EXP, SEQ], BF16)
        g_tab = sb("g_tab", [P, 3, P])
        g_fac = sb("g_fac", [P, 2, N_HEAD])
        g_xs = sb("g_xs", [P, DI])
        g_st = sb("g_st", [P, 4 * CHUNK])
        g_dec = sb("g_dec", [P, N_HEAD // 2])
        lent = conv[:, 1].rearrange("p m t -> p (m t)")
        xin = lent[:, 0:N_TILE * DM].rearrange("p (i d) -> p i d", i=N_TILE)
        base = N_TILE * DM
        sp_t, sp_l = (lent[:, base + 1024 * k:base + 1024 * (k + 1)] for k in range(2))
        sp_w = xtok[:, :, :].rearrange("p a c -> p (a c)")
        sp_m = ytok[:, :, :].rearrange("p a c -> p (a c)")
        early = yT[:, 0].rearrange("p m t -> p (m t)")
        sel32 = xv[0:3 * N_EXP, :, :].rearrange("p a c -> p (a c)")
        wmod = hs[:, :, :].rearrange("p e t -> p (e t)")[:, 0:KD * 6 * DM].rearrange("p (k n) -> p k n", k=KD)
        dt_f = dt[:, :, :].rearrange("p i h -> p (i h)")
        fu_f = fu[:, :, :].rearrange("p i h -> p (i h)")
        fv_f = fv[:, :, :].rearrange("p i h -> p (i h)")
        fq_f = fq[:, :, :].rearrange("p i h -> p (i h)")
        ident = cst[:, C_ID:C_ID + P]

        ld_x = [sem(f"ld_x{b}") for b in range(BATCH)]
        names = ["cst", "c", "wmod0", "wmod1", "win_x", "win_bc", "win_z", "win_dt", "early", "small", "wup", "ffn"]
        ld = {n: sem("ld_" + n) for n in names}
        ld_wo = sem("ld_wo")
        ld_wd = sem("ld_wd")
        ld_bd = sem("ld_bd")
        ld_res = [sem(f"ld_res{k}") for k in range(2)]
        full = [sem(f"bank{k}_full") for k in range(8)]
        consts_made = sem("consts_made")
        zeros_made = sem("zeros_made")
        warmed = sem("array_warmed_up")
        consts_cast = sem("consts_cast")
        csil_ready = sem("csil_ready")
        mod_ready = sem("mod_ready")
        gates_made = sem("gates_made")
        diag_ready = sem("diag_ready")
        gates_ready = sem("gates_ready")
        pool_chain = sem("pool_chain")
        dve_chain = sem("dve_chain")
        var_ready = sem("var_ready")
        rstd1_ready = sem("rstd1_ready")
        rstd_ready = sem("rstd_ready")
        xn_ready = sem("xn_ready")
        xn_used = sem("xn_used")
        hT_ready = sem("hT_ready")
        abs_ready = sem("abs_ready")
        relu_ready = sem("relu_ready")
        expt_ready = sem("expt_ready")
        onep_ready = sem("onep_ready")
        ln_ready = sem("ln_ready")
        dt_ready = sem("dt_ready")
        inverse_ready = sem("inverse_ready")
        q_ready = sem("q_ready")
        eclip_ready = sem("eclip_ready")
        uv_ready = sem("uv_ready")
        dec_ready = sem("dec_ready")
        clip_counted = sem("clip_counted")
        flag_ready = sem("flag_ready")
        tap0 = sem("tap0_written")
        taps = sem("taps_added")
        silu_done = sem("silu_done")
        sz_ready = sem("silu_z_ready")
        xtok_ready = sem("xtok_ready")
        btok_ready = sem("btok_ready")
        gm_ready = sem("gm_ready")
        xv_ready = sem("xv_ready")
        xq_ready = sem("xq_ready")
        st_ready = sem("st_ready")
        yo_done = sem("yo_done")
        lg_ready = sem("lg_ready")
        ytok_ready = sem("ytok_ready")
        ysum_ready = sem("ysum_ready")
        yT_ready = sem("yT_ready")
        x1_ready = sem("x1_ready")
        wog_ready = sem("wog_ready")
        wdg_ready = sem("wdg_ready")
        hid_ready = sem("hid_ready")
        th_ready = sem("th_ready")
        dl_ready = sem("dl_ready")
        tl_ready = sem("tl_ready")
        sc_ready = sem("sc_ready")
        sT_ready = sem("sT_ready")
        h_ready = sem("h_ready")
        hs_ready = sem("hs_ready")
        x2_ready = sem("x2_ready")
        g_table = sem("general_table_loaded")
        g_pe = sem("general_tensor_steps")
        g_act = sem("general_scalar_steps")
        g_dve = sem("general_vector_steps")
        stored = [sem(f"stored{k}") for k in range(2)]

        def bank(job):
            return ps[:, bank_of[job], :]

        def wait_bank(eng, job):
            eng.wait_ge(full[bank_of[job]], use_no[job] + 1)

        def done(eng, kind, tiles):
            if tiles > 0:
                where = divmod(tiles - 1, TPB)
                wait_bank(eng, (kind, 1) + where if kind == "y" else (kind,) + where)

        def halves(h):
            return slice(512 * h, 512 * h + 512)

        def tile_no(b, i):
            return b * TPB + i

        def chunks_before(b, i):
            return b * (2 * TPB - 1) + 2 * i

        def releases():
            when = {("mod", 0): (mod_ready, 1), ("mod", 1): (mod_ready, 3), "flag": (flag_ready, 1)}
            for b in range(BATCH):
                for k in range(KD):
                    when["hT", b, k] = (hT_ready, KD * b + k + 1)
                    when["hid", b, k] = (hid_ready, KD * b + k + 1)
                for m in range(N_PROJ):
                    when["proj", b, m] = ((taps, 3 * (N_CONV * b + m + 1)) if m < N_CONV
                                          else (sz_ready, CT_ * b + m - N_CONV + 1))
                when["gate1", b] = (th_ready, b + 1)
                when["gate2", b] = (lg_ready, b + 1)
                when["sT", b] = (sT_ready, 2 * b + 1)
                when["s3", b] = (sT_ready, 2 * b + 2)
                for e in range(N_EXP):
                    when["up", b, e] = (h_ready, N_EXP * b + e + 1)
                    when["bc", b, e] = (hs_ready, N_EXP * b + e + 1)
                for i in range(TPB):
                    n = tile_no(b, i)
                    when["xt", b, i] = (xtok_ready, n + 1)
                    when["bt", b, i] = (btok_ready, n + 1)
                    when["z", b, i] = (yT_ready, n + 1)
                    when["out", b, i] = (x1_ready, n + 1)
                    when["down", b, i] = (x2_ready, n + 1)
                    for a in range(2):
                        when["cb", a, b, i] = (gm_ready, 2 * n + a + 1)
                        when["st", a, b, i] = (st_ready, chunks_before(b, i) + a + 1)
                        when["y", a, b, i] = (ytok_ready, 2 * n + a + 1)
            for b in range(BATCH + 1):
                when["gates", b] = (gates_ready, b + 1)
            for h in range(2):
                when["dt", h] = (relu_ready, h + 1)
                when["E", h] = (clip_counted, h + 1)
            for n in range(4):
                when["D", n] = (dec_ready, 2 * n + 2)
            return when

        when_read = releases()
        before = {}
        for job in bank_of:
            for other in bank_of:
                if bank_of[other] == bank_of[job] and use_no[other] == use_no[job] - 1:
                    before[job] = other

        def wait_bank_free(pe, job):
            if job in before:
                pe.wait_ge(*when_read[before[job]])

        G_PRE = {"pe": 1, "act": 0, "dve": 2}
        G_LEVEL = {"pe": 5, "act": 1, "dve": 7}
        G_FIRST = {"pe": 2, "act": 3, "dve": 2}
        G_OTHER = {"pe": 4, "act": 3, "dve": 7}

        def g_before(engine, n):
            rows, i = divmod(n, TPB)
            tiles_first = rows + (1 if i else 0)
            return (n * (G_PRE[engine] + LEVELS * G_LEVEL[engine]) + tiles_first * G_FIRST[engine]
                    + (n - tiles_first) * G_OTHER[engine])

        g_bank = ps[:, G_BANK, :]

        def general_pe(pe, b, i):
            n = tile_no(b, i)
            p0, a0, d0 = (g_before(e, n) for e in ("pe", "act", "dve"))
            tok = slice(i * P, (i + 1) * P)
            pe.wait_ge(*when_read[g_after[b, i]])
            for j in range(CT_):
                ins = pe.transpose(g_bank[:, j * P:(j + 1) * P], conv[:, b % 2, j, tok], ident)
            ins.then_inc(g_pe, 1)
            p, a, d = p0 + G_PRE["pe"], a0 + G_PRE["act"], d0 + G_PRE["dve"]
            with pe.Fori(0, LEVELS) as lv:
                pe.wait_ge(g_dve, d + lv * G_LEVEL["dve"])
                pe.wait_ge(g_table, 16 * ((LEVELS + 1) * n + 1) + 16 * lv)
                for w in range(2):
                    ins = pe.matmul(g_bank[:, w * N_HEAD:(w + 1) * N_HEAD], g_tab[:, w, :], dt[:, n, :],
                                    start=True, stop=True)
                ins.then_inc(g_pe, 1)
                pe.wait_ge(g_act, a + 1 + lv * G_LEVEL["act"])
                for par in range(2):
                    if par:
                        pe.wait_ge(g_dve, d + 4 + lv * G_LEVEL["dve"])
                    rows = slice(64 * par, 64 * par + 64)
                    for j in range(CT_):
                        ins = pe.matmul(g_bank[:, j * P:(j + 1) * P], conv[rows, b % 2, CT_ + j, tok],
                                        conv[rows, b % 2, 2 * CT_ + j, tok], start=True, stop=True)
                    ins.then_inc(g_pe, 1)
                    pe.wait_ge(g_dve, d + 2 + 3 * par + lv * G_LEVEL["dve"])
                    for j in range(CT_):
                        g = 2 * j + par
                        ins = pe.matmul(g_bank[:, j * 64:(j + 1) * 64], g_gm(n)[:, j * P:(j + 1) * P],
                                        g_xs[:, g * 64:(g + 1) * 64], start=True, stop=True)
                    ins.then_inc(g_pe, 1)
            p, a, d = (p + LEVELS * G_LEVEL["pe"], a + LEVELS * G_LEVEL["act"], d + LEVELS * G_LEVEL["dve"])
            pe.wait_ge(g_dve, d)
            pe.wait_ge(g_table, 16 * (LEVELS + 1) * (n + 1))
            for w in range(3):
                ins = pe.matmul(g_bank[:, w * N_HEAD:(w + 1) * N_HEAD], g_tab[:, w, :], dt[:, n, :],
                                start=True, stop=True)
            ins.then_inc(g_pe, 1)
            pe.wait_ge(g_act, a + 3)
            pe.wait_ge(g_dve, d + 1)
            if i:
                for par in range(2):
                    if par:
                        pe.wait_ge(g_dve, d + 3)
                    rows = slice(64 * par, 64 * par + 64)
                    for j in range(CT_):
                        ins = pe.matmul(g_bank[:, j * 64:(j + 1) * 64], conv[rows, b % 2, 2 * CT_ + j, tok],
                                        g_st[rows, j * 64:(j + 1) * 64], start=True, stop=True)
                    ins.then_inc(g_pe, 1)
                pe.wait_ge(g_dve, d + 5)
            for g in range(N_GRP):
                j, par = g // 2, g % 2
                ins = pe.matmul(ps[64 * par:64 * par + 64, G_BANK, j * 64:(j + 1) * 64],
                                btok[:, n % 2, g * 64:(g + 1) * 64], g_xs[:, g * 64:(g + 1) * 64],
                                start=True, stop=True)
            ins.then_inc(g_pe, 1)
            pe.wait_ge(g_dve, g_before("dve", n + 1))

        def general_act(act, b, i):
            n = tile_no(b, i)
            p0, a0, d0 = (g_before(e, n) for e in ("pe", "act", "dve"))
            p, d = p0 + G_PRE["pe"], d0 + G_PRE["dve"]
            with act.Fori(0, LEVELS) as lv:
                act.wait_ge(g_dve, d + lv * G_LEVEL["dve"])
                act.dma_start(g_tab[:, :, :], g_src[bass.ds(lv, 1)].rearrange("o p w c -> (o p) w c")
                              ).then_inc(g_table, 16)
                act.wait_ge(g_pe, p + 1 + lv * G_LEVEL["pe"])
                act.activation(g_fac[:, :, :].rearrange("p w h -> p (w h)"), g_bank[:, 0:2 * N_HEAD], ACT.Exp,
                               scale=-1.0).then_inc(g_act, 1)
            p, d = p + LEVELS * G_LEVEL["pe"], d + LEVELS * G_LEVEL["dve"]
            act.wait_ge(g_dve, d)
            act.dma_start(g_tab[:, :, :], g_src[LEVELS]).then_inc(g_table, 16)
            act.wait_ge(g_pe, p + 1)
            act.activation(g_fac[:, :, :].rearrange("p w h -> p (w h)"), g_bank[:, 0:2 * N_HEAD], ACT.Exp,
                           scale=-1.0).then_inc(g_act, 1)
            for par in range(2):
                rows = slice(64 * par, 64 * par + 64)
                src = ps[rows, G_BANK, 2 * N_HEAD:3 * N_HEAD].rearrange("p (j a h) -> p a j h", a=2, h=8)[:, par]
                act.activation(g_dec[rows, :].rearrange("p (j h) -> p j h", h=8), src, ACT.Exp,
                               scale=-1.0).then_inc(g_act, 1)
            act.preload_act_table(ACT.Silu)
            act.wait_ge(g_dve, g_before("dve", n + 1))

        def general_dve(dve, b, i):
            n = tile_no(b, i)
            p0, a0, d0 = (g_before(e, n) for e in ("pe", "act", "dve"))
            xraw = xv[:, n % 2, :]
            y = ytok[:, n % 2, :]

            def scaled(w):
                return g_fac[:, w, :, None].to_broadcast([P, N_HEAD, HEAD])

            def add_y(par, count):
                yv = y.rearrange("p (j a h d) -> p a j h d", a=2, h=8, d=HEAD)[:, par]
                u = g_fac[:, 1, :].rearrange("p (j a h) -> p a j h", a=2, h=8)[:, par]
                part = scr[:, 0, :].rearrange("p (j h d) -> p j h d", h=8, d=HEAD)
                dve.tensor_tensor(part, g_bank[:, 0:256].rearrange("p (j h d) -> p j h d", h=8, d=HEAD),
                                  u[:, :, :, None].to_broadcast([P, CT_, 8, HEAD]), ALU.mult).then_inc(g_dve, 1)
                dve.wait_ge(g_dve, count + 1)
                y3 = y.rearrange("p (j a c) -> p a j c", a=2, c=64)[:, par]
                dve.tensor_tensor(y3, y3, scr[:, 0, :].rearrange("p (j c) -> p j c", c=64),
                                  ALU.add).then_inc(g_dve, 1)

            dve.wait_ge(ytok_ready, 2 * n + 2)
            dve.wait_ge(g_pe, p0 + 1)
            dve.tensor_copy(xraw, g_bank).then_inc(g_dve, 1)
            dve.memset(y, 0.0).then_inc(g_dve, 1)
            p, a, d = p0 + G_PRE["pe"], a0 + G_PRE["act"], d0 + G_PRE["dve"]
            dve.wait_ge(g_dve, d)
            with dve.Fori(0, LEVELS) as lv:
                ld_, lp = lv * G_LEVEL["dve"], lv * G_LEVEL["pe"]
                dve.wait_ge(g_dve, d + ld_)
                dve.wait_ge(g_act, a + 1 + lv * G_LEVEL["act"])
                dve.tensor_tensor(g_xs[:, :].rearrange("p (h d) -> p h d", d=HEAD),
                                  xraw.rearrange("p (h d) -> p h d", d=HEAD), scaled(0),
                                  ALU.mult).then_inc(g_dve, 1)
                for par in range(2):
                    dve.wait_ge(g_pe, p + 2 + 2 * par + lp)
                    dve.tensor_tensor(g_gm(n).rearrange("p (j s) -> p j s", s=P),
                                      g_bank.rearrange("p (j s) -> p j s", s=P),
                                      g_tab[:, 2:3, :].to_broadcast([P, CT_, P]), ALU.mult).then_inc(g_dve, 1)
                    dve.wait_ge(g_pe, p + 3 + 2 * par + lp)
                    add_y(par, d + 2 + 3 * par + ld_)
            p, a, d = (p + LEVELS * G_LEVEL["pe"], a + LEVELS * G_LEVEL["act"], d + LEVELS * G_LEVEL["dve"])
            dve.wait_ge(g_act, a + 3)
            dve.wait_ge(g_dve, d)
            dve.tensor_tensor(g_xs[:, :].rearrange("p (h d) -> p h d", d=HEAD),
                              xraw.rearrange("p (h d) -> p h d", d=HEAD), scaled(0), ALU.mult).then_inc(g_dve, 1)
            if i:
                for par in range(2):
                    dve.wait_ge(g_pe, p + 2 + par)
                    add_y(par, d + 1 + 2 * par)
                dve.wait_ge(g_pe, p + 4)
                s3v = g_st[:, :].rearrange("p (h d) -> p h d", d=HEAD)
                dve.tensor_tensor(s3v, s3v, g_dec[:, :, None].to_broadcast([P, N_HEAD // 2, HEAD]),
                                  ALU.mult).then_inc(g_dve, 1)
                dve.wait_ge(g_dve, d + 6)
                dve.tensor_tensor(g_st[:, :], g_st[:, :], g_bank[:, 0:256], ALU.add).then_inc(g_dve, 1)
            else:
                dve.wait_ge(g_pe, p + 2)
                dve.tensor_copy(g_st[:, :], g_bank[:, 0:256]).then_inc(g_dve, 1)
            dve.wait_ge(g_dve, g_before("dve", n + 1))

        def g_gm(n):
            return gm[:, n % 2].rearrange("p a c -> p (a c)")

        g_src = gen_d.rearrange("l p (w c) -> l p w c", w=3)

        block = ctx.enter_context(nc.Block())

        @block.sync
        def _(sp):
            xr = x_d.rearrange("b (i p) d -> b p i d", p=P)
            outr = out_d.rearrange("b (i p) d -> b p i d", p=P)
            wmod_r = wmod_d.rearrange("(k p) n -> p k n", p=P)
            win_r = win_d.rearrange("(k p) n -> p k n", p=P)

            def load_row(b):
                sp.dma_start(xin[:, b * TPB:(b + 1) * TPB, :], xr[b]).then_inc(ld_x[b], 16)

            def load_win(name, lo, hi):
                sp.dma_start(win[:, :, lo:hi], win_r[:, :, lo:hi]).then_inc(ld[name], 16)

            load_row(0)
            sp.dma_start(csb[:, :, :], cT_d.rearrange("(k p) b -> p k b", p=P)).then_inc(ld["c"], 16)
            sp.dma_start(cst[:, :], const_d).then_inc(ld["cst"], 16)
            sp.dma_start(wmod[:, :, 0:2 * DM], wmod_r[:, :, 0:2 * DM]).then_inc(ld["wmod0"], 16)
            sp.dma_start(small[:, :], small_d).then_inc(ld["small"], 16)
            load_row(1)
            load_win("win_x", 0, DI)
            load_row(2)
            load_row(3)
            load_win("win_dt", 4 * DI, N_IN)
            load_win("win_z", 3 * DI, 4 * DI)
            sp.dma_start(early, early_d).then_inc(ld["early"], 16)
            sp.dma_start(sel32, sel_d).then_inc(ld["early"], 16)
            sp.dma_start(wmod[:, :, 2 * DM:6 * DM], wmod_r[:, :, 2 * DM:6 * DM]).then_inc(ld["wmod1"], 16)
            load_win("win_bc", DI, 3 * DI)
            for t, d in ((wg1[:, :, :], wg1_d.rearrange("(k p) e -> p k e", p=P)), (wg2[:, :], wg2_d),
                         (bup[:, :], bup_d)):
                sp.dma_start(t, d).then_inc(ld["ffn"], 16)
            sp.dma_start(wup[:, :, :], wup_d.rearrange("(k p) n -> p k n", p=P)).then_inc(ld["wup"], 16)
            wo_r = wo_d.rearrange("(j p) n -> p j n", p=P)
            wd_r = wdn_d.rearrange("e p n -> p e n")

            def load_residual(b):
                sp.dma_start(x1[:, b % 2], xr[b]).then_inc(ld_res[b % 2], 16)

            def load_down(b):
                sp.dma_start(wdg[:, :, :], wd_r).then_inc(ld_wd, 16)
                sp.dma_start(bdg[:, :], bdn_d).then_inc(ld_bd, 16)

            def store_row(b):
                for i in range(TPB):
                    sp.wait_ge(x2_ready, tile_no(b, i) + 1)
                    sp.dma_start(outr[b][:, i, :], x1[:, b % 2, i, :]).then_inc(stored[b % 2], 16)

            sp.dma_start(wog[:, :, :], wo_r).then_inc(ld_wo, 16)
            load_residual(0)
            load_residual(1)
            load_down(0)
            for b in range(1, BATCH):
                done(sp, "out", TPB * b)
                sp.dma_start(wog[:, :, :], wo_r).then_inc(ld_wo, 16)
                if b >= 2:
                    store_row(b - 2)
                    done(sp, "down", TPB * (b - 1))
                    load_down(b - 1)
                    sp.wait_ge(stored[b % 2], 16 * TPB * (b // 2))
                    load_residual(b)
            store_row(BATCH - 2)
            done(sp, "down", TPB * (BATCH - 1))
            load_down(BATCH - 1)
            store_row(BATCH - 1)
            for k in range(2):
                sp.wait_ge(stored[k], 16 * TPB * (BATCH // 2))

        @block.gpsimd
        def _(pool):
            chain = [0]

            def link(ins):
                chain[0] += 1
                ins.then_inc(pool_chain, 1)
                pool.wait_ge(pool_chain, chain[0])

            def rstd(n):
                pool.wait_ge(var_ready, n + 1)
                link(pool.tensor_scalar(rst[:, n % 2], mv[:, n % 2, 1:2], EPS, None, ALU.add))
                pool.tensor_tensor(rst[:, n % 2], rst[:, n % 2], half[:, 0:1], ALU.pow).then_inc(rstd_ready, 1)

            pool.memset(half[:, :], -0.5).then_inc(consts_made, 1)
            pool.wait_ge(consts_made, 1)
            for step in STEPS:
                kind = step[0]
                if kind == "ln1":
                    b = step[1]
                    r = rst1[:, b * TPB:(b + 1) * TPB, :]
                    pool.wait_ge(var_ready, TPB * (b + 1))
                    link(pool.tensor_scalar(r, mv1[:, b * TPB:(b + 1) * TPB, 1:2], EPS, None, ALU.add))
                    pool.tensor_tensor(r, r, half[:, 0:1, None].to_broadcast([P, TPB, 1]),
                                       ALU.pow).then_inc(rstd1_ready, 1)
                elif kind == "d_dt":
                    h = step[1]
                    fq_h = fq[:, 8 * h:8 * h + 8, :]
                    pool.wait_ge(ld["small"], 16)
                    pool.wait_ge(inverse_ready, h + 1)
                    pool.tensor_tensor(fq_h, fq_h, dh.rearrange("p (o h) -> p o h", o=1).to_broadcast([P, 8, N_HEAD]),
                                       ALU.mult).then_inc(q_ready, 1)
                elif kind == "mod" and step[1] == 1:
                    pool.wait_ge(mod_ready, 4)
                    for a, which in enumerate((2, 5)):
                        g = modT[:, which * KD:(which + 1) * KD, :]
                        sgn = gsg[:, a]
                        link(pool.tensor_scalar(sgn, g, 0.0, 2.0, ALU.is_ge, ALU.mult))
                        link(pool.tensor_scalar(sgn, sgn, 1.0, None, ALU.subtract))
                        link(pool.tensor_tensor(g, g, sgn, ALU.mult))
                        link(pool.tensor_scalar(g, g, 0.25, None, ALU.max))
                        pool.tensor_tensor(g, g, sgn, ALU.mult).then_inc(gates_made, 1)
                elif kind == "tr":
                    b, i = step[1:]
                    n = tile_no(b, i)
                    r = n % 2
                    pool.wait_ge(uv_ready, 4)
                    pool.wait_ge(q_ready, n // 8 + 1)
                    pool.wait_ge(xtok_ready, n + 1)
                    if n == 0:
                        pool.wait_ge(consts_cast, 1)
                    if n >= 2:
                        done(pool, "y", n - 1)
                    xh = xtok[:, r].rearrange("p (h d) -> p h d", d=HEAD)
                    pool.tensor_tensor(xv[:, r].rearrange("p (h d) -> p h d", d=HEAD), xh,
                                       fv[:, n, :, None].to_broadcast([P, N_HEAD, HEAD]),
                                       ALU.mult).then_inc(xv_ready, 1)
                    pool.wait_ge(xv_ready, n + 1)
                    pool.tensor_tensor(xh, xh, fq[:, n, :, None].to_broadcast([P, N_HEAD, HEAD]),
                                       ALU.mult).then_inc(xq_ready, 1)
                elif kind == "norm":
                    rstd(N_TILE + tile_no(*step[1:]))
                elif kind == "fold_out":
                    b = step[1]
                    pool.wait_ge(gates_ready, b + 1)
                    pool.wait_ge(ld_wo, 16 * (b + 1))
                    pool.tensor_tensor(wog[:, :, :], wog[:, :, :], gates[:, 0:1, :].to_broadcast([P, CT_, DM]),
                                       ALU.mult).then_inc(wog_ready, 1)
                elif kind == "fold_down":
                    b = step[1]
                    pool.wait_ge(ld_wd, 16 * (b + 1))
                    pool.wait_ge(ld_bd, 16 * (b + 1))
                    pool.wait_ge(gates_ready, b + 2)
                    pool.tensor_tensor(wdg[:, :, :], wdg[:, :, :],
                                       gates[:, 1:2, :].to_broadcast([P, N_EXP, DM]),
                                       ALU.mult).then_inc(wdg_ready, 1)
                    pool.tensor_tensor(bdg[:, :], bdg[:, :], gates[0:N_EXP, 1, :],
                                       ALU.mult).then_inc(wdg_ready, 1)

        @block.scalar
        def _(act):
            pending = []
            hold_silu = False

            def silu_conv():
                b, m = pending.pop(0)
                act.wait_ge(taps, 3 * (N_CONV * b + m + 1))
                dst = conv[:, b % 2, m, :]
                act.activation(dst, dst, ACT.Silu).then_inc(silu_done, 1)

            out_of_range = [None]
            act.wait_ge(ld["c"], 16)
            act.activation(csil[:, :, :], csb[:, :, :], ACT.Silu).then_inc(csil_ready, 1)
            for step in STEPS:
                kind = step[0]
                if kind == "ln1":
                    b = step[1]
                    act.wait_ge(mod_ready, 2)
                    for k in range(KD):
                        wait_bank(act, ("hT", b, k))
                        act.activation(hT[:, k, b * SEQ:(b + 1) * SEQ], bank(("hT", b, k)), ACT.Identity,
                                       bias=modT[:, k, b:b + 1],
                                       scale=modT[:, KD + k, b:b + 1]).then_inc(hT_ready, 1)
                elif kind == "mod" and step[1] == 1:
                    act.wait_ge(ld["cst"], 16)
                    act.wait_ge(ld["early"], 32)
                    act.activation(sel[:, :, :].rearrange("p e c -> p (e c)"), sel32, ACT.Copy).then_inc(consts_cast, 1)
                    act.activation(identb[:, :], ident, ACT.Copy).then_inc(consts_cast, 1)
                elif kind == "abs":
                    h = step[1]
                    wait_bank(act, ("dt", h))
                    act.activation(sp_t[:, halves(h)], bank(("dt", h)), ACT.Abs).then_inc(abs_ready, 1)
                elif kind == "exp":
                    h = step[1]
                    hold_silu = True
                    act.wait_ge(abs_ready, h + 1)
                    act.activation(sp_t[:, halves(h)], sp_t[:, halves(h)], ACT.Exp,
                                   scale=-1.0).then_inc(expt_ready, 1)
                    if h == 1:
                        for h in range(2):
                            act.wait_ge(onep_ready, h + 1)
                            act.activation(sp_l[:, halves(h)], sp_w[:, halves(h)], ACT.Ln).then_inc(ln_ready, 1)
                elif kind == "factors":
                    h = step[1]
                    s = halves(h)
                    act.wait_ge(eclip_ready, h + 1)
                    act.activation(fu_f[:, s], sp_l[:, s], ACT.Exp, scale=-1.0).then_inc(uv_ready, 1)
                    act.activation(fv_f[:, s], sp_l[:, s], ACT.Exp).then_inc(uv_ready, 1)
                elif kind == "flag":
                    hold_silu = False
                    act.wait_ge(flag_ready, 1)
                    out_of_range[0] = act.value_load(flag[0:1, 0:1])
                elif kind == "decays":
                    for n in range(4):
                        which, h = n // 2, n % 2
                        wait_bank(act, ("D", n))
                        cnt = 8 if n < 3 else 7
                        for par in range(2):
                            rows = slice(64 * par, 64 * par + 64)
                            src = ps[rows, bank_of[("D", n)], 0:cnt * N_HEAD].rearrange(
                                "p (i j a h) -> p i j a h", j=CT_, a=2, h=8)[:, :, :, par, :]
                            dst = dec[rows, 8 * h:8 * h + cnt, which, :].rearrange("p i (j h) -> p i j h", h=8)
                            ins = act.activation(dst, src, ACT.Exp, scale=-1.0)
                            ins.then_inc(dec_ready, 1)
                elif kind == "proj":
                    b, m = step[1:]
                    wait_bank(act, step)
                    if (b, m) == (0, N_CONV):
                        act.wait_ge(ld["small"], 16)
                    if m == 0:
                        if b >= 2:
                            done(act, "y", TPB * (b - 1))
                        if b == 1:
                            act.wait_ge(xn_ready, N_TILE)
                            act.wait_ge(clip_counted, 2)
                            act.wait_ge(uv_ready, 4)
                            act.wait_ge(consts_cast, 2)
                            act.wait_ge(dec_ready, 8)
                    if m < N_CONV:
                        act.activation(conv[:, b % 2, m, :], bank(step), ACT.Identity, bias=cb[:, m:m + 1],
                                       scale=cw[:, m, KSIZE - 1:KSIZE]).then_inc(tap0, 1)
                    else:
                        if m == N_CONV and b:
                            act.wait_ge(yT_ready, TPB * b)
                        act.activation(sz[:, m - N_CONV, :], bank(step), ACT.Silu,
                                       bias=zb[:, m - N_CONV:m - N_CONV + 1]).then_inc(sz_ready, 1)
                    while pending and not hold_silu:
                        silu_conv()
                    if m < N_CONV:
                        pending.append((b, m))
                elif kind == "gates":
                    b = step[1]
                    wait_bank(act, step)
                    if b >= 1:
                        act.wait_ge(wog_ready, b)
                    if b >= 2:
                        act.wait_ge(wdg_ready, 2 * (b - 1))
                    lo, hi = (DM if b == BATCH else 0), (DM if b == 0 else 2 * DM)
                    act.activation(gates[:, :, :].rearrange("p a d -> p (a d)")[:, lo:hi], bank(step)[:, lo:hi],
                                   ACT.Copy).then_inc(gates_ready, 1)
                elif kind == "tr":
                    b, i = step[1:]
                    n = tile_no(b, i)
                    while i == 0 and pending:
                        silu_conv()
                    wait_bank(act, ("xt", b, i))
                    if n == 0:
                        act.wait_ge(clip_counted, 2)
                    if n >= 2:
                        act.wait_ge(ysum_ready, n - 1)
                    act.activation(xtok[:, n % 2, :], bank(("xt", b, i)), ACT.Copy).then_inc(xtok_ready, 1)
                elif kind == "bt":
                    b, i = step[1:]
                    n = tile_no(b, i)
                    wait_bank(act, step)
                    if n >= 2:
                        done(act, "y", n - 1)
                    act.activation(btok[:, n % 2, :], bank(("bt", b, i)), ACT.Copy).then_inc(btok_ready, 1)
                elif kind == "y":
                    with act.If(out_of_range[0] > 0):
                        general_act(act, *step[1:])
                elif kind == "hid":
                    b = step[1]
                    act.wait_ge(mod_ready, 4)
                    for k in range(KD):
                        wait_bank(act, ("hid", b, k))
                        act.activation(hT[:, k, b * SEQ:(b + 1) * SEQ], bank(("hid", b, k)), ACT.Identity,
                                       bias=modT[:, 3 * KD + k, b:b + 1],
                                       scale=modT[:, 4 * KD + k, b:b + 1]).then_inc(hid_ready, 1)
                elif kind == "gate1":
                    wait_bank(act, step)
                    done(act, "down", TPB * step[1])
                    act.activation(th[:, :], bank(step)[0:N_EXP, :], ACT.Tanh).then_inc(th_ready, 1)
                elif kind == "gate2":
                    b = step[1]
                    wait_bank(act, step)
                    if b >= 1:
                        act.wait_ge(sc_ready, b)
                    act.activation(lg[:, :, :].rearrange("p i e -> p (i e)"), bank(step)[:, 0:TPB * N_EXP],
                                   ACT.Copy).then_inc(lg_ready, 1)
                elif kind == "score":
                    b = step[1]
                    act.wait_ge(dl_ready, b + 1)
                    act.activation(tl[:, :, :], dl[:, :, :], ACT.Tanh, scale=0.5).then_inc(tl_ready, 1)
                elif kind == "spread":
                    b = step[1]
                    if b >= 1:
                        done(act, "down", TPB * b)
                    act.wait_ge(lg_ready, b + 1)
                    wait_bank(act, ("sT", b))
                    act.activation(sT[:, :], bank(("sT", b))[0:N_EXP, :], ACT.Copy).then_inc(sT_ready, 1)
                    wait_bank(act, ("s3", b))
                    act.activation(s3T[:, :], bank(("s3", b))[0:3 * N_EXP, 0:256].bitcast(BF16),
                                   ACT.Copy).then_inc(sT_ready, 1)
                elif kind == "up":
                    b, e = step[1:]
                    wait_bank(act, step)
                    if (b, e) == (0, 0):
                        act.wait_ge(ld["ffn"], 48)
                    if b >= 1 and e == 0:
                        done(act, "down", TPB * b)
                    act.activation(hs[:, e, :], bank(step), ACT.Silu, bias=bup[:, e:e + 1]).then_inc(h_ready, 1)

        @block.vector
        def _(dve):
            chain = [0]

            def link(ins):
                chain[0] += 1
                ins.then_inc(dve_chain, 1)
                dve.wait_ge(dve_chain, chain[0])

            def stats(src, n):
                if n >= 2:
                    dve.wait_ge(xn_ready, n - 1)
                link(dve.bn_stats(bns[:, n % 2, :], src))
                dve.bn_aggr(mv[:, n % 2, :], bns[:, n % 2, :]).then_inc(var_ready, 1)

            def row_stats(b):
                dve.wait_ge(ld_x[b], 16)
                for i in range(TPB):
                    chain[0] += 1
                    dve.bn_stats(bns1[:, b % 2, i, :], xin[:, tile_no(b, i), :]).then_inc(dve_chain, 1)
                for i in range(TPB):
                    dve.wait_ge(dve_chain, chain[0] - TPB + 1 + i)
                    dve.bn_aggr(mv1[:, tile_no(b, i), :], bns1[:, b % 2, i, :]).then_inc(var_ready, 1)

            def normalize(src, n):
                if n < N_TILE:
                    mean, rstd = mv1[:, n, 0:1], rst1[:, n, 0:1]
                    dve.wait_ge(rstd1_ready, n // TPB + 1)
                else:
                    mean, rstd = mv[:, n % 2, 0:1], rst[:, n % 2, 0:1]
                    dve.wait_ge(rstd_ready, n - N_TILE + 1)
                dve.wait_ge(var_ready, n + 1)
                if n >= 4:
                    group, i = divmod(n - 4, TPB)
                    if i < TPB - 1:
                        dve.wait_ge(xn_used, (TPB - 1) * group + i + 1)
                    else:
                        wait_bank(dve, ("hT", group, 1) if group < BATCH else ("hid", group - BATCH, 1))
                dve.tensor_scalar(xn[:, n % 4, :], src, mean, rstd,
                                  ALU.subtract, ALU.mult).then_inc(xn_ready, 1)

            out_of_range = [None]
            pending = []

            def older_taps():
                b, m = pending.pop()
                c = N_CONV * b + m
                dve.wait_ge(tap0, c + 1)
                for s in range(1, KSIZE):
                    if s > 1:
                        dve.wait_ge(taps, 3 * c + s - 1)
                    dst = conv[:, b % 2, m, s:SEQ]
                    dve.scalar_tensor_tensor(
                        out=dst, in0=bank(("proj", b, m))[:, 0:SEQ - s], scalar=cw[:, m, KSIZE - 1 - s:KSIZE - s],
                        in1=dst, op0=ALU.mult, op1=ALU.add).then_inc(taps, 1)

            dve.memset(g_xs[:, :], 0.0).then_inc(zeros_made, 1)
            row_stats(0)
            for step in STEPS:
                kind = step[0]
                if pending and (kind == "proj" or kind == "tr" and step[2] == 0):
                    older_taps()
                due = bool(pending)
                if kind == "mod":
                    half_no = step[1]
                    wait_bank(dve, step)
                    lo, hi = MOD_TILES[half_no]
                    dve.tensor_copy(modT[:, lo:hi, :].rearrange("p m b -> p (m b)"),
                                    bank(step)[:, lo * BATCH:hi * BATCH]).then_inc(mod_ready, 1)
                    dve.wait_ge(mod_ready, 2 * half_no + 1)
                    which = (1, 4)[half_no]
                    m = modT[:, which * KD:(which + 1) * KD, :]
                    dve.tensor_scalar(m, m, 1.0, None, ALU.add).then_inc(mod_ready, 1)
                elif kind == "ln1":
                    b = step[1]
                    for i in range(TPB):
                        n = tile_no(b, i)
                        normalize(xin[:, n, :], n)
                    if b + 1 < BATCH:
                        row_stats(b + 1)
                elif kind == "exp":
                    h = step[1]
                    s = halves(h)
                    dve.wait_ge(expt_ready, h + 1)
                    dve.tensor_scalar(sp_w[:, s], sp_t[:, s], 1.0, None, ALU.add).then_inc(onep_ready, 1)
                    dve.wait_ge(onep_ready, h + 1)
                    link(dve.scalar_tensor_tensor(out=sp_m[:, s], in0=sp_w[:, s], scalar=1.0, in1=sp_t[:, s],
                                                  op0=ALU.subtract, op1=ALU.subtract))
                    dve.scalar_tensor_tensor(out=sp_m[:, s], in0=bank(("dt", h)), scalar=0.0, in1=sp_m[:, s],
                                             op0=ALU.max, op1=ALU.subtract).then_inc(relu_ready, 1)
                elif kind == "log":
                    h = step[1]
                    dve.wait_ge(ln_ready, h + 1)
                    dve.wait_ge(relu_ready, h + 1)
                    dve.tensor_tensor(dt_f[:, halves(h)], sp_l[:, halves(h)], sp_m[:, halves(h)],
                                      ALU.add).then_inc(dt_ready, 1)
                elif kind == "factors":
                    h = step[1]
                    s = halves(h)
                    wait_bank(dve, ("E", h))
                    dve.wait_ge(dt_ready, h + 1)
                    dve.tensor_scalar(sp_l[:, s], bank(("E", h)), -RANGE, RANGE, ALU.max,
                                      ALU.min).then_inc(eclip_ready, 1)
                    dve.wait_ge(eclip_ready, h + 1)
                    dve.scalar_tensor_tensor(out=sp_w[:, s], in0=bank(("E", h)), scalar=1.0, in1=sp_l[:, s],
                                             op0=ALU.mult, op1=ALU.not_equal,
                                             accum_out=flg[:, h:h + 1]).then_inc(clip_counted, 1)
                elif kind == "diag":
                    b = step[1]
                    if b:
                        dve.wait_ge(st_ready, chunks_before(b, 0))
                    dve.wait_ge(gates_made, 2)
                    for a, (which, row) in enumerate(((2, b), (5, b - 1))):
                        if not 0 <= row < BATCH:
                            continue
                        for k in range(KD):
                            dve.tensor_scalar(scr[:, a, k * P:(k + 1) * P], ident,
                                              modT[:, which * KD + k, row:row + 1], None,
                                              ALU.mult).then_inc(diag_ready, 1)
                elif kind == "gates":
                    wait_bank(dve, step)
                elif kind == "flag":
                    wait_bank(dve, "flag")
                    link(dve.tensor_reduce(flsum[:, :], bank("flag")[:, 0:2], AX.X, ALU.add))
                    dve.tensor_copy(flag[:, :], flsum[0:1, :]).then_inc(flag_ready, 1)
                    dve.wait_ge(flag_ready, 1)
                    out_of_range[0] = dve.value_load(flag[0:1, 0:1])
                elif kind == "d_dt":
                    h = step[1]
                    dve.wait_ge(dt_ready, h + 1)
                    dve.reciprocal(fq_f[:, halves(h)], dt_f[:, halves(h)]).then_inc(inverse_ready, 1)
                elif kind == "proj" and step[2] < N_CONV:
                    pending.append(step[1:])
                elif kind == "tr":
                    b, i = step[1:]
                    n = tile_no(b, i)
                    if n >= 2:
                        done(dve, "y", n - 1)
                    for par in range(2):
                        job = ("cb", par, b, i)
                        wait_bank(dve, job)
                        dve.tensor_tensor(
                            gm[:, n % 2, par].rearrange("p (j s) -> p j s", s=CHUNK),
                            bank(job)[:, 0:4 * CHUNK].rearrange("p (j s) -> p j s", s=CHUNK),
                            cst[:, None, C_TRI:C_TRI + CHUNK].to_broadcast([P, 4, CHUNK]),
                            ALU.mult).then_inc(gm_ready, 1)
                elif kind == "state":
                    b, i = step[1:]
                    n = tile_no(b, i)
                    for c in range(2):
                        job = ("st", c, b, i)
                        if job not in bank_of:
                            continue
                        k = chunks_before(b, i) + c
                        wait_bank(dve, job)
                        d = dec[:, n, c, :, None].to_broadcast([P, 32, HEAD])
                        new = st[:, k % 4, :].rearrange("p (h d) -> p h d", d=HEAD)
                        if n >= 1:
                            done(dve, "y", n)
                        pst = bank(job)[:, 0:4 * CHUNK]
                        dve.wait_ge(dec_ready, 8)
                        if i == 0 and c == 0:
                            dve.tensor_tensor(new, pst.rearrange("p (h d) -> p h d", d=HEAD), d,
                                              ALU.mult).then_inc(st_ready, 1)
                        else:
                            dve.wait_ge(st_ready, k)
                            link(dve.tensor_tensor(scr[:, 0, :], pst, st[:, (k - 1) % 4, :], ALU.add))
                            dve.tensor_tensor(new, scr[:, 0, :].rearrange("p (h d) -> p h d", d=HEAD), d,
                                              ALU.mult).then_inc(st_ready, 1)
                elif kind == "y":
                    b, i = step[1:]
                    n = tile_no(b, i)
                    if n >= 2:
                        done(dve, "z", n - 1)
                    for par in range(2):
                        job = ("y", par, b, i)
                        wait_bank(dve, job)
                        dst = ytok[:, n % 2, :].rearrange("p (j a h d) -> p a j h d", a=2, h=8, d=HEAD)[:, par]
                        u = fu[:, n, :].rearrange("p (j a h) -> p a j h", a=2, h=8)[:, par]
                        dve.tensor_tensor(dst, bank(job)[:, 0:4 * CHUNK].rearrange("p (j h d) -> p j h d", h=8, d=HEAD),
                                          u[:, :, :, None].to_broadcast([P, CT_, 8, HEAD]),
                                          ALU.mult).then_inc(ytok_ready, 1)
                    with dve.If(out_of_range[0] > 0):
                        general_dve(dve, b, i)
                    dve.wait_ge(xq_ready, n + 1)
                    dve.wait_ge(ytok_ready, 2 * n + 2)
                    dve.tensor_tensor(ytok[:, n % 2, :], ytok[:, n % 2, :], xtok[:, n % 2, :],
                                      ALU.add).then_inc(ysum_ready, 1)
                elif kind == "z":
                    b, i = step[1:]
                    n = tile_no(b, i)
                    wait_bank(dve, step)
                    if n >= 2:
                        done(dve, "out", n - 1)
                    dve.wait_ge(sz_ready, CT_ * (b + 1))
                    dve.tensor_tensor(yT[:, n % 2], bank(step)[:, :].rearrange("p (m t) -> p m t", t=P),
                                      sz[:, :, i * P:(i + 1) * P],
                                      ALU.mult).then_inc(yT_ready, 1)
                elif kind == "out":
                    b, i = step[1:]
                    n = tile_no(b, i)
                    wait_bank(dve, step)
                    dve.wait_ge(ld_res[b % 2], 16 * (b // 2 + 1))
                    r = x1[:, b % 2, i, :]
                    dve.tensor_tensor(r, bank(step)[:, 0:DM], r, ALU.add).then_inc(x1_ready, 1)
                    dve.wait_ge(x1_ready, n + 1)
                    stats(r, N_TILE + n)
                elif kind == "norm":
                    b, i = step[1:]
                    normalize(x1[:, b % 2, i, :], N_TILE + tile_no(b, i))
                elif kind == "gate2":
                    b = step[1]
                    dve.wait_ge(lg_ready, b + 1)
                    for i in range(TPB):
                        ins = dve.max(top[:, i, :], lg[:, i, :])
                        chain[0] += 1
                        ins.then_inc(dve_chain, 1)
                    mine = lg[:, :, :, None].to_broadcast([P, TPB, N_EXP, N_EXP])
                    other = lg[:, :, None, :].to_broadcast([P, TPB, N_EXP, N_EXP])
                    for dst, op in ((cmp_, ALU.is_gt), (eq, ALU.is_equal)):
                        ins = dve.tensor_tensor(dst[:, :, :, :], other, mine, op)
                        chain[0] += 1
                        ins.then_inc(dve_chain, 1)
                    dve.wait_ge(dve_chain, chain[0])
                    tri8 = cst[:, None, C_RANK:C_RANK + 64].to_broadcast([P, TPB, 64])
                    eqf = eq[:, :, :, :].rearrange("p i a b -> p i (a b)")
                    cmf = cmp_[:, :, :, :].rearrange("p i a b -> p (i a b)")
                    link(dve.tensor_tensor(eqf, eqf, tri8, ALU.mult))
                    link(dve.tensor_tensor(cmf, cmf, eq[:, :, :, :].rearrange("p i a b -> p (i a b)"), ALU.add))
                    link(dve.tensor_reduce(rank[:, :, :].rearrange("p i a -> p (i a)"),
                                           cmp_[:, :, :, :].rearrange("p i a b -> p (i a) b"), AX.X, ALU.add))
                    link(dve.tensor_scalar(rank[:, :, :], rank[:, :, :], 1.5, 0.5, ALU.is_lt, ALU.mult))
                    link(dve.tensor_tensor(msum[:, :], top[:, :, 0], top[:, :, 1], ALU.add))
                    dve.scalar_tensor_tensor(out=dl[:, :, :], in0=lg[:, :, :], scalar=2.0,
                                             in1=msum[:, :, None].to_broadcast([P, TPB, N_EXP]),
                                             op0=ALU.mult, op1=ALU.subtract).then_inc(dl_ready, 1)
                elif kind == "score":
                    b = step[1]
                    dve.wait_ge(tl_ready, b + 1)
                    link(dve.scalar_tensor_tensor(out=sc[:, :, :], in0=tl[:, :, :], scalar=1.0, in1=rank[:, :, :],
                                                  op0=ALU.add, op1=ALU.mult))
                    link(dve.tensor_copy(s3[:, :, 0, :], sc[:, :, :]))
                    link(dve.tensor_tensor(dl[:, :, :], sc[:, :, :], s3[:, :, 0, :], ALU.subtract))
                    link(dve.tensor_copy(s3[:, :, 1, :], dl[:, :, :]))
                    dve.tensor_tensor(s3[:, :, 2, :], dl[:, :, :], s3[:, :, 1, :], ALU.subtract).then_inc(sc_ready, 1)
                elif kind == "bc":
                    b, e = step[1:]
                    wait_bank(dve, step)
                    dve.wait_ge(h_ready, b * N_EXP + e + 1)
                    dve.tensor_tensor(hs[:, e, :], hs[:, e, :], bank(step), ALU.mult).then_inc(hs_ready, 1)
                elif kind == "down":
                    b, i = step[1:]
                    n = tile_no(b, i)
                    wait_bank(dve, step)
                    r = x1[:, b % 2, i, :]
                    dve.wait_ge(xn_ready, N_TILE + n + 1)
                    dve.tensor_tensor(r, bank(step)[:, 0:DM], r, ALU.add).then_inc(x2_ready, 1)
                if due and pending:
                    older_taps()

        @block.tensor
        def _(pe):
            def tile_cols(i):
                return slice(i * P, (i + 1) * P)

            def transpose_norm(b, name):
                first = 0 if name == "hT" else N_TILE
                for i in range(TPB):
                    n = first + tile_no(b, i)
                    pe.wait_ge(xn_ready, n + 1)
                    for k in range(KD):
                        job = (name, b, k)
                        if i == 0:
                            wait_bank_free(pe, job)
                        ins = pe.transpose(bank(job)[:, tile_cols(i)], xn[:, n % 4, k * P:(k + 1) * P], ident)
                        if i == TPB - 1:
                            ins.then_inc(full[bank_of[job]], 1)
                        elif k == KD - 1:
                            ins.then_inc(xn_used, 1)

            def to_tokens(job, base):
                b, i = job[1:]
                wait_bank_free(pe, job)
                for j in range(CT_):
                    ins = pe.transpose(bank(job)[:, tile_cols(j)], conv[:, b % 2, base + j, tile_cols(i)], ident)
                ins.then_inc(full[bank_of[job]], 1)

            out_of_range = [None]
            pe.wait_ge(zeros_made, 1)
            for _ in range(WARM_UP):
                ins = pe.matmul(ps[:, WARM_BANK, :], g_xs[:, 0:P], g_xs[:, :], start=True, stop=True)
            ins.then_inc(warmed, 1)
            pe.wait_ge(warmed, 1)
            pe.wait_ge(ld["cst"], 16)
            for step in STEPS:
                kind = step[0]
                if kind == "mod":
                    pe.wait_ge(ld[("wmod0", "wmod1")[step[1]]], 16)
                    pe.wait_ge(csil_ready, 1)
                    wait_bank_free(pe, step)
                    for m in range(*MOD_TILES[step[1]]):
                        for k in range(KD):
                            ins = pe.matmul(bank(step)[:, m * BATCH:(m + 1) * BATCH], wmod[:, k, m * P:(m + 1) * P],
                                            csil[:, k, :], start=(k == 0), stop=(k == KD - 1))
                    ins.then_inc(full[bank_of[step]], 1)
                elif kind == "ln1":
                    transpose_norm(step[1], "hT")
                elif kind == "dt":
                    h = step[1]
                    job = ("dt", h)
                    pe.wait_ge(ld["win_dt"], 16)
                    wait_bank_free(pe, job)
                    for i in range(8):
                        n = 8 * h + i
                        pe.wait_ge(hT_ready, KD * (n // TPB + 1))
                        for k in range(KD):
                            ins = pe.matmul(bank(job)[:, i * N_HEAD:(i + 1) * N_HEAD], hT[:, k, tile_cols(n)],
                                            win[:, k, 4 * DI:N_IN], start=(k == 0), stop=(k == KD - 1))
                    ins.then_inc(full[bank_of[job]], 1)
                elif kind == "factors":
                    h = step[1]
                    job = ("E", h)
                    pe.wait_ge(dt_ready, h + 1)
                    pe.wait_ge(ld["early"], 32)
                    wait_bank_free(pe, job)
                    pe.matmul(bank(job), early[:, E_MID:E_MID + P], dt_f[:, 512 * h:512 * h + 512],
                              start=True, stop=True).then_inc(full[bank_of[job]], 1)
                elif kind == "decays":
                    pe.wait_ge(dt_ready, 2)
                    for n in range(4):
                        job = ("D", n)
                        wait_bank_free(pe, job)
                        lo = 512 * (n % 2)
                        cnt = 512 if n < 3 else 448
                        if n < 2:
                            ins = pe.matmul(bank(job), early[:, E_AB:E_AB + P], dt_f[:, lo:lo + cnt], start=True, stop=True)
                        else:
                            pe.matmul(bank(job)[:, 0:cnt], early[:, E_BH:E_BH + P], dt_f[:, lo:lo + cnt],
                                      start=True, stop=False)
                            ins = pe.matmul(bank(job)[:, 0:cnt], early[:, E_AL:E_AL + P],
                                            dt_f[:, lo + N_HEAD:lo + N_HEAD + cnt], start=False, stop=True)
                        ins.then_inc(full[bank_of[job]], 1)
                elif kind == "flag":
                    pe.wait_ge(clip_counted, 2)
                    wait_bank_free(pe, "flag")
                    pe.matmul(bank("flag")[:, 0:2], cst[:, C_ONE:C_ONE + P], flg[:, :],
                              start=True, stop=True).then_inc(full[bank_of["flag"]], 1)
                    pe.wait_ge(flag_ready, 1)
                    out_of_range[0] = pe.value_load(flag[0:1, 0:1])
                elif kind == "proj":
                    b, m = step[1:]
                    wait_bank_free(pe, step)
                    if b == 0 and m in (0, CT_, N_CONV):
                        pe.wait_ge(ld[{0: "win_x", CT_: "win_bc", N_CONV: "win_z"}[m]], 16)
                    pe.wait_ge(hT_ready, KD * (b + 1))
                    for k in range(KD):
                        ins = pe.matmul(bank(step), win[:, k, m * P:(m + 1) * P], hT[:, k, b * SEQ:(b + 1) * SEQ],
                                        start=(k == 0), stop=(k == KD - 1))
                    ins.then_inc(full[bank_of[step]], 1)
                elif kind == "gates":
                    b = step[1]
                    wait_bank_free(pe, step)
                    made = KD * (2 * b + 1) if b < BATCH else 2 * KD * b
                    pe.wait_ge(diag_ready, made)
                    for a, row in enumerate((b, b - 1)):
                        if not 0 <= row < BATCH:
                            continue
                        for k in range(KD):
                            ins = pe.matmul(bank(step)[:, a * DM + k * P:a * DM + (k + 1) * P],
                                            cst[:, C_ONE:C_ONE + P], scr[:, a, k * P:(k + 1) * P],
                                            start=True, stop=True)
                    ins.then_inc(full[bank_of[step]], 1)
                elif kind == "tr":
                    b, i = step[1:]
                    pe.wait_ge(silu_done, N_CONV * (b + 1))
                    to_tokens(("xt", b, i), 0)
                    for par in range(2):
                        rows = slice(64 * par, 64 * par + 64)
                        job = ("cb", par, b, i)
                        wait_bank_free(pe, job)
                        for j in range(CT_):
                            for c in range(2):
                                t = slice(i * P + c * CHUNK, i * P + (c + 1) * CHUNK)
                                ins = pe.matmul(
                                    ps[64 * c:64 * c + 64, bank_of[job], j * CHUNK:(j + 1) * CHUNK],
                                    conv[rows, b % 2, CT_ + j, t], conv[rows, b % 2, 2 * CT_ + j, t],
                                    start=True, stop=True)
                        ins.then_inc(full[bank_of[job]], 1)
                elif kind == "bt":
                    to_tokens(step, CT_)
                elif kind == "state":
                    b, i = step[1:]
                    n = tile_no(b, i)
                    pe.wait_ge(btok_ready, n + 1)
                    pe.wait_ge(xv_ready, n + 1)
                    for c in range(2):
                        job = ("st", c, b, i)
                        if job not in bank_of:
                            continue
                        rows = slice(64 * c, 64 * c + 64)
                        wait_bank_free(pe, job)
                        for g in range(N_GRP):
                            j, par = g // 2, g % 2
                            ins = pe.matmul(ps[64 * par:64 * par + 64, bank_of[job], j * CHUNK:(j + 1) * CHUNK],
                                            btok[rows, n % 2, g * 64:(g + 1) * 64],
                                            xv[rows, n % 2, g * 64:(g + 1) * 64], start=True, stop=True)
                        ins.then_inc(full[bank_of[job]], 1)
                elif kind == "y":
                    b, i = step[1:]
                    n = tile_no(b, i)
                    pe.wait_ge(gm_ready, 2 * n + 2)
                    pe.wait_ge(st_ready, chunks_before(b, i) + 1)
                    for par in range(2):
                        wait_bank_free(pe, ("y", par, b, i))
                    for par in range(2):
                        rows = slice(64 * par, 64 * par + 64)
                        for c in range(2):
                            if i == 0 and c == 0:
                                continue
                            k = chunks_before(b, i) + c - 1
                            t = slice(i * P + c * CHUNK, i * P + (c + 1) * CHUNK)
                            for j in range(CT_):
                                ins = pe.matmul(
                                    ps[64 * c:64 * c + 64, bank_of[("y", par, b, i)], j * CHUNK:(j + 1) * CHUNK],
                                    conv[rows, b % 2, 2 * CT_ + j, t], st[rows, k % 4, j * CHUNK:(j + 1) * CHUNK],
                                    start=(j == 0), stop=False, skip_group_check=True)
                        ins.then_inc(yo_done, 1)
                    for par in range(2):
                        job = ("y", par, b, i)
                        pe.wait_ge(yo_done, 2 * n + par + 1)
                        for c in range(2):
                            rows = slice(64 * c, 64 * c + 64)
                            for j in range(CT_):
                                g = 2 * j + par
                                last = pe.matmul(
                                    ps[rows, bank_of[job], j * CHUNK:(j + 1) * CHUNK],
                                    gm[rows, n % 2, par, j * CHUNK:(j + 1) * CHUNK],
                                    xv[rows, n % 2, g * 64:(g + 1) * 64],
                                    start=(i == 0 and c == 0 and j == 0), stop=True, skip_group_check=True)
                        if par == 0:
                            last.then_inc(full[bank_of[job]], 1)
                    job = ("y", 1, b, i)
                    last.then_inc(full[bank_of[job]], 1)
                    with pe.If(out_of_range[0] > 0):
                        general_pe(pe, b, i)
                elif kind == "z":
                    b, i = step[1:]
                    n = tile_no(b, i)
                    wait_bank_free(pe, step)
                    pe.wait_ge(ysum_ready, n + 1)
                    for m in range(CT_):
                        ins = pe.transpose(bank(step)[:, tile_cols(m)], ytok[:, n % 2, tile_cols(m)], ident)
                    ins.then_inc(full[bank_of[step]], 1)
                elif kind == "out":
                    b, i = step[1:]
                    n = tile_no(b, i)
                    wait_bank_free(pe, step)
                    pe.wait_ge(yT_ready, n + 1)
                    pe.wait_ge(wog_ready, b + 1)
                    for m in range(CT_):
                        ins = pe.matmul(bank(step)[:, 0:DM], yT[:, n % 2, m, :], wog[:, m, :],
                                        start=(m == 0), stop=(m == CT_ - 1))
                    ins.then_inc(full[bank_of[step]], 1)
                elif kind == "hid":
                    transpose_norm(step[1], "hid")
                elif kind == "gate1":
                    b = step[1]
                    wait_bank_free(pe, step)
                    pe.wait_ge(hid_ready, KD * (b + 1))
                    pe.wait_ge(ld["ffn"], 48)
                    for k in range(KD):
                        ins = pe.matmul(bank(step)[0:N_EXP, :], wg1[:, k, :], hT[:, k, b * SEQ:(b + 1) * SEQ],
                                        start=(k == 0), stop=(k == KD - 1))
                    ins.then_inc(full[bank_of[step]], 1)
                elif kind == "gate2":
                    b = step[1]
                    wait_bank_free(pe, step)
                    pe.wait_ge(th_ready, b + 1)
                    for i in range(TPB):
                        ins = pe.matmul(bank(step)[:, i * N_EXP:(i + 1) * N_EXP], th[:, tile_cols(i)], wg2[:, :],
                                        start=True, stop=True)
                    ins.then_inc(full[bank_of[step]], 1)
                elif kind == "spread":
                    b = step[1]
                    pe.wait_ge(sc_ready, b + 1)
                    job = ("sT", b)
                    wait_bank_free(pe, job)
                    for i in range(TPB):
                        ins = pe.transpose(bank(job)[0:N_EXP, tile_cols(i)], sc[:, i, :], ident)
                    ins.then_inc(full[bank_of[job]], 1)
                    job = ("s3", b)
                    wait_bank_free(pe, job)
                    pe.wait_ge(consts_cast, 2)
                    dst = bank(job)[0:3 * N_EXP, 0:256].bitcast(BF16)
                    for i in range(TPB):
                        ins = pe.transpose(dst[:, tile_cols(i)], s3[:, i].rearrange("p a e -> p (a e)"), identb[:, :])
                    ins.then_inc(full[bank_of[job]], 1)
                elif kind == "up":
                    b, e = step[1:]
                    wait_bank_free(pe, step)
                    pe.wait_ge(ld["wup"], 16)
                    pe.wait_ge(hid_ready, KD * (b + 1))
                    for k in range(KD):
                        ins = pe.matmul(bank(step), wup[:, k, e * P:(e + 1) * P], hT[:, k, b * SEQ:(b + 1) * SEQ],
                                        start=(k == 0), stop=(k == KD - 1))
                    ins.then_inc(full[bank_of[step]], 1)
                elif kind == "bc":
                    b, e = step[1:]
                    wait_bank_free(pe, step)
                    pe.wait_ge(sT_ready, 2 * b + 2)
                    pe.matmul(bank(step), sel[:, e, :], s3T[:, :], start=True, stop=True).then_inc(
                        full[bank_of[step]], 1)
                elif kind == "down":
                    b, i = step[1:]
                    wait_bank_free(pe, step)
                    pe.wait_ge(wdg_ready, 2 * (b + 1))
                    out = bank(step)[:, 0:DM]
                    pe.matmul(out, sT[:, tile_cols(i)], bdg[:, :], start=True, stop=False)
                    for e in range(N_EXP):
                        pe.wait_ge(hs_ready, b * N_EXP + e + 1)
                        ins = pe.matmul(out, hs[:, e, tile_cols(i)], wdg[:, e, :], start=False, stop=(e == N_EXP - 1))
                    ins.then_inc(full[bank_of[step]], 1)


def _shape_constants():
    import numpy as np
    c = np.zeros((P, C_ALL), np.float32)
    early = np.zeros((P, E_ALL), np.float32)
    k = np.arange(P)[:, None]
    t = np.arange(P)[None, :]
    c[:, C_ID:C_ID + P] = np.eye(P)
    same = k // CHUNK == t // CHUNK
    kk, tt, mid = k % CHUNK, t % CHUNK, CHUNK // 2
    early[:, E_MID:E_MID + P] = same * (((tt >= mid) & (kk >= mid) & (kk <= tt)) * 1.0
                                    - ((tt < mid) & (kk < mid) & (kk > tt)) * 1.0)
    rows = np.arange(P)[:, None] * np.ones((1, P))
    early[:, E_AB:E_AB + P] = (rows >= mid) & (rows < CHUNK + mid)
    early[:, E_BH:E_BH + P] = rows >= CHUNK + mid
    early[:, E_AL:E_AL + P] = rows < mid
    c[:, C_TRI:C_TRI + CHUNK] = (k % CHUNK) <= np.arange(CHUNK)[None, :]
    s = np.zeros((P, N_EXP, P), np.float32)
    for e in range(N_EXP):
        for part in range(3):
            s[part * N_EXP + e, e, :] = 1.0
    sel = s[0:3 * N_EXP].reshape(3 * N_EXP, N_EXP * P)
    e = np.arange(N_EXP)
    c[:, C_RANK:C_RANK + 64] = (e[None, :] < e[:, None]).astype(np.float32).reshape(1, 64)
    c[:, C_ONE:C_ONE + P] = 1.0
    return c, early, sel


def _general_tables():
    import numpy as np
    k = np.arange(P)[:, None]
    t = np.arange(P)[None, :]
    g = np.zeros((LEVELS + 1, P, 3, P), np.float32)
    for lv in range(LEVELS - 1):
        size = P >> (lv + 1)
        ref = t // (2 * size) * (2 * size) + size - 1
        later = t // size % 2 == 1
        w = (later & (k > ref) & (k <= t)) | (~later & (k > t) & (k <= ref))
        g[lv, :, 0] = g[lv, :, 1] = w
        g[lv, :, 2] = (k // (2 * size) == t // (2 * size)) & (k // size % 2 == 0) & later
    g[LEVELS - 1, :, 2] = k == t
    g[LEVELS, :, 0] = k > t
    g[LEVELS, :, 1] = k <= t
    g[LEVELS, :, 2] = 1.0
    return g.reshape(LEVELS + 1, P, 3 * P)


def kernel(**inputs):
    import numpy as np
    import concourse.bacc as bacc
    from concourse.bass_utils import run_bass_kernel_spmd

    a = {k: np.asarray(v) for k, v in inputs.items()}
    cont = np.ascontiguousarray

    def by_tile(v):
        return cont(np.moveaxis(v.reshape((-1, P) + v.shape[1:]), 0, 1))

    arrays = {
        "x": cont(a["L0_attn_input_"]),
        "c_T": cont(a["L0_c"].T),
        "w_mod": cont(a["L0_wmod"]),
        "w_in_T": cont(a["L0_attn_in_proj_w"].T),
        "small_params": cont(np.concatenate([
            by_tile(a["L0_attn_conv1d_weight"][:, 0, :]).reshape(P, -1), by_tile(a["L0_attn_conv1d_bias"]),
            by_tile(a["L0_attn_z_bias"]), np.broadcast_to(a["L0_attn_D"], (P, N_HEAD))], axis=1)),
        "w_out_T": cont(a["L0_attn_out_proj_w"].T),
        "w_g1_T": cont(a["L0_ffn_Wg1"].T),
        "w_g2_T": cont(a["L0_ffn_Wg2"].T),
        "w_up_T": cont(a["L0_ffn_Wup"].reshape(N_EXP * D_EXP, DM).T),
        "b_up": cont(a["L0_ffn_bup"].T),
        "w_down_T": cont(a["L0_ffn_Wdown"].transpose(0, 2, 1)),
        "b_down": cont(a["L0_ffn_bdown"]),
        "shape_consts": _shape_constants()[0],
        "early_consts": _shape_constants()[1],
        "expert_rows": _shape_constants()[2],
        "general_tables": _general_tables(),
    }
    nc = bacc.Bacc("TRN2", target_bir_lowering=False, num_devices=1)
    args = [nc.dram_tensor(n, v.shape, mybir.dt.from_np(v.dtype), kind="ExternalInput").ap()
            for n, v in arrays.items()]
    args.append(nc.dram_tensor("out", (BATCH, SEQ, DM), F32, kind="ExternalOutput").ap())
    adaln_block(nc, *args)
    r = run_bass_kernel_spmd(nc, [arrays], core_ids=[0])
    return r.results[0]["out"]
```
